# Optimizing a Trainium2 kernel written in Bass

```python
import numpy as np
import jax
import jax.numpy as jnp

def _softmax(x, axis=-1):
    return jax.nn.softmax(x, axis=axis)

def _gelu(x):
    return jax.nn.gelu(x, approximate=True)

def _silu(x):
    return jax.nn.silu(x)

def _sigmoid(x):
    return jax.nn.sigmoid(x)

def _layernorm(x, axis=-1, eps=1e-05):
    m = jnp.mean(x, axis=axis, keepdims=True)
    v = jnp.var(x, axis=axis, keepdims=True)
    return (x - m) / jnp.sqrt(v + eps)

def _scatter_add(tgt, idx, src, axis=0):
    return tgt.at[idx].add(src)

def _segment_sum(src, seg, n):
    return jax.ops.segment_sum(src, seg, n)
kernel_name = 'mk_seq_preln_d1_jaxref_r4_8f208d'

def setup_inputs(seed: int=0):
    np.random.seed(seed)
    _w = jnp.asarray

    def _L0_attn_setup():
        import jax, jax.numpy as jnp
        import numpy as np
        DIM = 256
        B, T = (4, 1024)
        CAP = 10.0
        EPS_N = 1e-06
        EPS_RMS = 1e-08

        def softcap(x, a=CAP):
            return a * jnp.tanh(x / a)
        key = jax.random.key(seed)
        k1, k2 = jax.random.split(key)
        x = jax.random.normal(k1, (B, T, DIM), dtype=jnp.float32)
        W = jax.random.normal(k2, (DIM, 4 * DIM), dtype=jnp.float32) / np.sqrt(DIM)
        b = jnp.zeros((4 * DIM,), dtype=jnp.float32)
        input_bias = -jnp.ones((DIM,), dtype=jnp.float32)
        scale = jnp.ones((DIM,), dtype=jnp.float32)
        return {'x': x, 'W': W, 'b': b, 'input_bias': input_bias, 'scale': scale}
    _L0_attn_in = _L0_attn_setup()

    def _L0_ffn_setup():
        import jax, jax.numpy as jnp
        import numpy as np
        B, S, H, F, G = (8, 512, 256, 1024, 128)
        EPS = 1e-05

        def _dequant(q, scales, g):
            K, N = q.shape
            w = (q.astype(jnp.float32) - 128.0).reshape(K // g, g, N) * scales[:, None, :]
            return w.reshape(K, N)
        key = jax.random.key(seed)
        ks = jax.random.split(key, 8)
        x = jax.random.normal(ks[0], (B, S, H), dtype=jnp.float32)
        ln_gamma = jnp.ones((H,), jnp.float32)
        ln_beta = jnp.zeros((H,), jnp.float32)
        fc1_q = jax.random.randint(ks[1], (H, F), 0, 64, dtype=jnp.int32)
        fc2_q = jax.random.randint(ks[2], (F, H), 0, 64, dtype=jnp.int32)
        fc1_scales = jax.random.uniform(ks[3], (H // G, F), jnp.float32) * 0.02 + 0.001
        fc2_scales = jax.random.uniform(ks[4], (F // G, H), jnp.float32) * 0.02 + 0.001
        fc1_bias = jax.random.normal(ks[5], (F,), jnp.float32) * 0.02
        fc2_bias = jax.random.normal(ks[6], (H,), jnp.float32) * 0.02
        return {'x': x, 'ln_gamma': ln_gamma, 'ln_beta': ln_beta, 'fc1_q': fc1_q, 'fc1_scales': fc1_scales, 'fc1_bias': fc1_bias, 'fc2_q': fc2_q, 'fc2_scales': fc2_scales, 'fc2_bias': fc2_bias}
    _L0_ffn_in = _L0_ffn_setup()
    _d = {'L0_attn_x': _L0_attn_in['x'], 'L0_attn_W': _L0_attn_in['W'], 'L0_attn_b': _L0_attn_in['b'], 'L0_attn_input_bias': _L0_attn_in['input_bias'], 'L0_attn_scale': _L0_attn_in['scale'], 'L0_ffn_ln_gamma': _L0_ffn_in['ln_gamma'], 'L0_ffn_ln_beta': _L0_ffn_in['ln_beta'], 'L0_ffn_fc1_q': _L0_ffn_in['fc1_q'], 'L0_ffn_fc1_scales': _L0_ffn_in['fc1_scales'], 'L0_ffn_fc1_bias': _L0_ffn_in['fc1_bias'], 'L0_ffn_fc2_q': _L0_ffn_in['fc2_q'], 'L0_ffn_fc2_scales': _L0_ffn_in['fc2_scales'], 'L0_ffn_fc2_bias': _L0_ffn_in['fc2_bias']}
    _x0 = _d['L0_attn_x']
    _d['L0_attn_x'] = jax.random.normal(jax.random.fold_in(jax.random.key(seed), 1), (2, 2048, 256), dtype=_x0.dtype)
    del _x0
    return _d

def reference(L0_attn_x, L0_attn_W, L0_attn_b, L0_attn_input_bias, L0_attn_scale, L0_ffn_ln_gamma, L0_ffn_ln_beta, L0_ffn_fc1_q, L0_ffn_fc1_scales, L0_ffn_fc1_bias, L0_ffn_fc2_q, L0_ffn_fc2_scales, L0_ffn_fc2_bias):

    def _L0_attn_ref(x, W, b, input_bias, scale):
        import jax, jax.numpy as jnp
        import numpy as np
        DIM = 256
        B, T = (4, 1024)
        CAP = 10.0
        EPS_N = 1e-06
        EPS_RMS = 1e-08

        def softcap(x, a=CAP):
            return a * jnp.tanh(x / a)
        pre = jnp.einsum('btd,df->btf', x, W) + b
        i_pre, f_pre, o_pre, z = jnp.split(pre, 4, axis=-1)
        i_gate = softcap(i_pre + input_bias)
        f_gate = -jax.nn.softplus(f_pre)
        o_sig = jax.nn.sigmoid(o_pre)
        tz = jnp.tanh(z)
        seq = (jnp.swapaxes(i_gate, 0, 1), jnp.swapaxes(f_gate, 0, 1), jnp.swapaxes(o_sig, 0, 1), jnp.swapaxes(tz, 0, 1))
        c0 = jnp.zeros((x.shape[0], DIM), dtype=x.dtype)
        n0 = jnp.zeros_like(c0)
        m0 = jnp.zeros_like(c0)

        def step(carry, inp):
            c, n, m = carry
            i_t, f_t, o_t, tz_t = inp
            m_next = jnp.maximum(f_t + m, i_t)
            i_s = jnp.exp(i_t - m_next)
            f_s = jnp.exp(f_t + m - m_next)
            c = f_s * c + i_s * tz_t
            n = f_s * n + i_s
            h = o_t * (c / (n + EPS_N))
            return ((c, n, m_next), h)
        _, hs = jax.lax.scan(step, (c0, n0, m0), seq)
        out = jnp.swapaxes(hs, 0, 1)
        rms = jnp.sqrt(jnp.mean(jnp.square(out), axis=-1, keepdims=True) + EPS_RMS)
        out = out / rms * scale
        return out

    def _L0_ffn_ref(x, ln_gamma, ln_beta, fc1_q, fc1_scales, fc1_bias, fc2_q, fc2_scales, fc2_bias):
        import jax, jax.numpy as jnp
        import numpy as np
        B, S, H, F, G = (8, 512, 256, 1024, 128)
        EPS = 1e-05

        def _dequant(q, scales, g):
            K, N = q.shape
            w = (q.astype(jnp.float32) - 128.0).reshape(K // g, g, N) * scales[:, None, :]
            return w.reshape(K, N)
        residual = x
        mu = jnp.mean(x, axis=-1, keepdims=True)
        var = jnp.mean(jnp.square(x - mu), axis=-1, keepdims=True)
        h = (x - mu) * jax.lax.rsqrt(var + EPS) * ln_gamma + ln_beta
        hf = h.reshape(-1, H)
        w1 = _dequant(fc1_q, fc1_scales, G)
        y = hf @ w1 + fc1_bias
        y = jax.nn.silu(y)
        w2 = _dequant(fc2_q, fc2_scales, G)
        z = y @ w2 + fc2_bias
        return residual + 0.5 * z.reshape(residual.shape)
    x = L0_attn_x
    x = x + _L0_attn_ref(_layernorm(x, axis=-1), L0_attn_W, L0_attn_b, L0_attn_input_bias, L0_attn_scale)
    x = x + _L0_ffn_ref(_layernorm(x, axis=-1), L0_ffn_ln_gamma, L0_ffn_ln_beta, L0_ffn_fc1_q, L0_ffn_fc1_scales, L0_ffn_fc1_bias, L0_ffn_fc2_q, L0_ffn_fc2_scales, L0_ffn_fc2_bias)
    return x

_drawn_inputs = setup_inputs


def setup_inputs(seed=0):
    import zlib

    import numpy as np

    out = dict(_drawn_inputs(seed))
    spreads = {'L0_attn_b': (0.0, 0.1),
     'L0_attn_input_bias': (-1.0, 0.2),
     'L0_attn_scale': (1.0, 0.2),
     'L0_ffn_ln_gamma': (1.0, 0.2),
     'L0_ffn_ln_beta': (0.0, 0.1)}
    factors = {}
    for name, (base, spread) in spreads.items():
        noise = np.random.default_rng([zlib.crc32(name.encode()), seed]).standard_normal(out[name].shape)
        drawn = base * np.exp(spread * noise) if base else spread * noise
        out[name] = jnp.asarray(drawn.astype(out[name].dtype))
    for name, factor in factors.items():
        out[name] = (out[name] * factor).astype(out[name].dtype)
    return out
```

```python
from contextlib import ExitStack

import concourse.bass as bass
from concourse import mybir

F32 = mybir.dt.float32
F32R = mybir.dt.float32r
I32 = mybir.dt.int32
ALU = mybir.AluOpType
ACT = mybir.ActivationFunctionType

P = 128
SEQS, STEPS, D = 2, 2048, 256
GATES, F = 4 * D, 1024
T = 512
TT = T // P
CHUNKS = SEQS * STEPS // T
KD = D // P
KF = F // P
GJ = GATES // P
CAP = 10.0
EPS_N, EPS_RMS, EPS_LN = 1e-6, 1e-8, 1e-5
ZERO_POINT = 128.0
GATE_ORDER = [0, 1, 2, 3, 6, 7, 4, 5]
I_TILES, F_TILES, Z_TILES, O_TILES = (0, 1), (2, 3), (4, 5), (6, 7)
COL_B, COL_IB, COL_GAMMA, COL_BETA, COL_B1 = 0, GJ, GJ + KD, GJ + 2 * KD, GJ + 3 * KD
COLS = COL_B1 + KF
LOOP_FROM, LOOP_TO = 3, 7
LAST_SLOT = CHUNKS + 1


class Chunk:

    def __init__(self, at, reg=None):
        self.at, self.reg = at, reg

    def __add__(self, n):
        return Chunk(self.at + n, self.reg)

    def __sub__(self, n):
        return self + -n

    @property
    def exists(self):
        return 0 <= self.at < CHUNKS

    @property
    def seq(self):
        return self.at % SEQS

    def block(self):
        return self.at // SEQS if self.reg is None else self.reg + self.at // SEQS

    def count(self, per, k):
        n = per * self.at + k
        return n if self.reg is None else self.reg * (2 * per) + n

    def of_seq(self, per):
        n = per * (self.at // SEQS + 1)
        return n if self.reg is None else self.reg * per + n


def run_slots(eng, slot):
    for t in range(LOOP_FROM):
        slot(Chunk(t))
    with eng.Fori(0, (LOOP_TO - LOOP_FROM) // 2) as i:
        slot(Chunk(LOOP_FROM, i))
        slot(Chunk(LOOP_FROM + 1, i))
    for t in range(LOOP_TO, LAST_SLOT + 1):
        slot(Chunk(t))


def early_h(t):
    return t.reg is None and t.at >= CHUNKS - 1


def wait_apart(eng, semaphore, n, passed):
    eng.wait_ge(semaphore, n)
    eng.sem_inc(passed, 1)


def layer(nc, x, w_gates, cols, scale_row, fc1_q, fc1_scales, fc2_q, fc2_scales, b2_row, out):
    x_view = x.rearrange("s (c t p) d -> s c p t d", t=TT, p=P)
    out_view = out.rearrange("s (c t p) d -> s c p t d", t=TT, p=P)

    with ExitStack() as ctx:
        def sb(name, shape, dt=F32):
            return ctx.enter_context(nc.sbuf_tensor(name, shape, dt))

        def ps(name, shape):
            return ctx.enter_context(nc.psum_tensor(name, shape, F32))

        def sem(name):
            return ctx.enter_context(nc.semaphore(name))

        wg_hi = sb("wg_hi", [P, KD, GATES], F32R)
        wg_lo = sb("wg_lo", [P, KD, GATES], F32R)
        w1_hi = sb("w1_hi", [P, KD, F], F32R)
        w1_lo = sb("w1_lo", [P, KD, F], F32R)
        w2_hi = sb("w2_hi", [P, KF, D], F32R)
        w2_lo = sb("w2_lo", [P, KF, D], F32R)
        wg_raw = sb("wg_raw", [P, KD, GATES])
        q1 = sb("q1", [P, KD, F], I32)
        q2 = sb("q2", [P, KF, D], I32)
        s1 = sb("s1", [P, KD, F])
        s2 = wg_raw[:].rearrange("p k (h d) -> p (k h) d", d=D)
        w1_f = q1[:].bitcast(F32)
        w2_f = q2[:].bitcast(F32)
        ident = sb("ident", [P, P])
        col = sb("col", [P, COLS])
        gate_bias = sb("gate_bias", [P, GJ])
        b1_all = sb("b1_all", [P, KF])
        scale_bc = sb("scale_bc", [P, D])
        b2_bc = sb("b2_bc", [P, D])
        x_in = sb("x_in", [P, 2, TT, D])
        xn = sb("xn", [P, TT, D])
        g = sb("g", [P, TT, D])
        base = sb("base", [P, 2, TT, D])
        out_sb = sb("out_sb", [P, 2, 2, D])
        xt_hi = sb("xt_hi", [P, KD, T], F32R)
        xt_lo = sb("xt_lo", [P, KD, T], F32R)
        gt_hi = sb("gt_hi", [P, KD, T], F32R)
        gt_lo = sb("gt_lo", [P, KD, T], F32R)
        y = sb("y", [P, 3, T])
        y_hi = sb("y_hi", [P, KF, T], F32R)
        y_lo = sb("y_lo", [P, KF, T], F32R)
        rec = [sb(f"rec{s}", [P, 3, KD, T]) for s in range(2)]
        f_gate = sb("f_gate", [P, 2, KD, T])
        o_gate = sb("o_gate", [P, 2, KD, T])
        carry = sb("carry", [P, 2, 3, KD])
        bn1 = sb("bn1", [P, TT, 6])
        mv1 = sb("mv1", [P, TT, 2])
        ve1 = sb("ve1", [P, 2, TT])
        nm1 = sb("nm1", [P, 2, TT])
        r1 = sb("r1", [P, TT])
        nr1 = sb("nr1", [P, TT])
        bn2 = sb("bn2", [P, TT, 6])
        mv2 = sb("mv2", [P, TT, 2])
        ve2 = sb("ve2", [P, 2, 2, TT])
        nm2 = sb("nm2", [P, 2, TT])
        r2 = sb("r2", [P, 2, TT])
        nr2 = sb("nr2", [P, 2, TT])
        up2 = sb("up2", [P, TT])
        sumsq = sb("sumsq", [P, 2, TT])
        meansq = sb("meansq", [P, 2, TT])
        rrms = sb("rrms", [P, 2, TT])
        minus_half = sb("minus_half", [P, 2 * TT])

        mm_ps = ps("mm_ps", [P, 4, T])
        z_ps = ps("z_ps", [P, 2, 2, D])
        t_ps = ps("t_ps", [P, 2, T])

        ident_ready = sem("ident_ready")
        half_ready = sem("half_ready")
        wg_in, q1_in, q2_in, s1_in, col_in, row_in = (sem(n) for n in (
            "wg_in", "q1_in", "q2_in", "s1_in", "col_in", "row_in"))
        s2_in = sem("s2_in")
        bias_ready = sem("bias_ready")
        carry_zeroed = sem("carry_zeroed")
        wg_split_hi, wg_split_lo = sem("wg_split_hi"), sem("wg_split_lo")
        w1_step, w2_step = sem("w1_step"), sem("w2_step")
        beta_w1 = sem("beta_w1")
        b1_ready = sem("b1_ready")
        x_landed = [sem(f"x_landed{s}") for s in range(2)]
        res_landed = [sem(f"res_landed{s}") for s in range(2)]
        out_landed = [sem(f"out_landed{u}") for u in range(2)]
        ln1_stat = sem("ln1_stat")
        ln1_norm = sem("ln1_norm")
        xt_ready = sem("xt_ready")
        xt_hi_done = sem("xt_hi_done")
        xt_lo_done = sem("xt_lo_done")
        pre_done = sem("pre_done")
        gate_done = sem("gate_done")
        i_ready = sem("i_ready")
        iz_ready = sem("iz_ready")
        scan_done = sem("scan_done")
        denom_ready = sem("denom_ready")
        recip_done = sem("recip_done")
        oc_ready = sem("oc_ready")
        h_done = sem("h_done")
        ht_ready = sem("ht_ready")
        sq_done = sem("sq_done")
        ms_ready = sem("ms_ready")
        rrms_ready = sem("rrms_ready")
        hs_done = sem("hs_done")
        x1_done = sem("x1_done")
        ln2_stat = sem("ln2_stat")
        ln2_norm = sem("ln2_norm")
        gt_ready = sem("gt_ready")
        gt_hi_done = sem("gt_hi_done")
        gt_lo_done = sem("gt_lo_done")
        fc1_done = sem("fc1_done")
        silu_done = sem("silu_done")
        y_hi_done = sem("y_hi_done")
        y_lo_done = sem("y_lo_done")
        fc2_done = sem("fc2_done")
        final_done = sem("final_done")

        sp_passed, dve_passed, pool_passed = sem("sp_passed"), sem("dve_passed"), sem("pool_passed")

        block = ctx.enter_context(nc.Block())

        @block.sync
        def _(sp):
            def load_x(c):
                if c.at >= 2:
                    wait_apart(sp, ln1_norm, (c - 2).count(6, 6), sp_passed)
                sp.dma_start(x_in[:, c.seq], x_view[c.seq, bass.ds(c.block(), 1)].rearrange("c p t d -> (c p) t d")
                             ).then_inc(x_landed[c.seq], 16)

            sp.dma_start(x_in[:, 0], x_view[0, 0]).then_inc(x_landed[0], 16)
            for k in range(KD):
                sp.dma_start(wg_raw[:, k], w_gates[k * P:(k + 1) * P, :]).then_inc(wg_in, 16)
            sp.dma_start(x_in[:, 1], x_view[1, 0]).then_inc(x_landed[1], 16)
            sp.dma_start(q1[:], fc1_q.rearrange("(k p) f -> p k f", p=P)).then_inc(q1_in, 16)
            sp.dma_start(s1[:], fc1_scales.partition_broadcast(P)).then_inc(s1_in, 16)
            sp.dma_start(q2[:], fc2_q.rearrange("(k p) f -> p k f", p=P)).then_inc(q2_in, 16)
            sp.wait_ge(wg_split_lo, KD)
            sp.dma_start(s2, fc2_scales.partition_broadcast(P)).then_inc(s2_in, 16)

            def slot(t):
                if (t + 1).exists and not (t.reg is None and t.at == 0):
                    load_x(t + 1)
                c = t - 2
                if c.exists:
                    for u in range(2):
                        wait_apart(sp, final_done, c.count(2, u + 1), sp_passed)
                        sp.dma_start(
                            out_view[c.seq, bass.ds(c.block(), 1), :, 2 * u:2 * u + 2].rearrange("c p t d -> (c p) t d"),
                            out_sb[:, u]).then_inc(out_landed[u], 16)
                if t.exists:
                    sp.dma_start(base[:, t.seq], x_view[t.seq, bass.ds(t.block(), 1)].rearrange("c p t d -> (c p) t d")
                                 ).then_inc(res_landed[t.seq], 16)

            run_slots(sp, slot)
            for u in range(2):
                sp.wait_ge(out_landed[u], 16 * CHUNKS)

        @block.tensor
        def _(pe):
            def three_passes(dst, w_pair, w_at, a_pair, a_at, first, last):
                (wh, wl), (ah, al) = w_pair, a_pair
                pe.matmul(dst, wh[w_at], ah[a_at], start=first, stop=False)
                pe.matmul(dst, wh[w_at], al[a_at], start=False, stop=False)
                return pe.matmul(dst, wl[w_at], ah[a_at], start=False, stop=last)

            def turn_back(src, ready):
                for k in range(KD):
                    yield k
                    for n in range(TT):
                        ins = pe.transpose(t_ps[:, k, n * P:(n + 1) * P], src[:, n, k * P:(k + 1) * P], ident[:])
                    ins.then_inc(ready, 1)

            def x_turned(c):
                pe.wait_ge(ln1_norm, c.count(6, 6))
                for k in turn_back(xn, xt_ready):
                    if c.at >= 3:
                        pe.wait_ge(gt_lo_done, (c - 3).count(2, k + 1))
                    elif c.at >= 1:
                        pe.wait_ge(xt_lo_done, (c - 1).count(2, k + 1))

            def g_turned(c):
                pe.wait_ge(ln2_norm, c.count(13, 8))
                for k in turn_back(g, gt_ready):
                    pe.wait_ge(hs_done, c.count(4, 2 * k + 2))

            def h_turned(c):
                pe.wait_ge(h_done, c.count(3, 3))
                for u in range(2):
                    if (c + 2).exists:
                        pe.wait_ge(xt_lo_done, (c + 2).count(2, u + 1))
                    else:
                        pe.wait_ge(gt_lo_done, (c - 1).count(2, u + 1))
                    for n in range(2):
                        for k in range(KD):
                            at = (2 * n + k) * P
                            tok = (2 * u + n) * P
                            ins = pe.transpose(t_ps[:, u, at:at + P], rec[c.seq][:, 0, k, tok:tok + P], ident[:])
                    ins.then_inc(ht_ready, 1)

            def gate_products(c, tiles):
                if 0 in tiles:
                    pe.wait_ge(xt_lo_done, c.count(2, 2))
                for j in tiles:
                    if j >= 4:
                        pe.wait_ge(gate_done, c.count(8, j - 3))
                    elif c.at >= 3:
                        pe.wait_ge(silu_done, (c - 3).count(8, j + 5))
                    elif c.at >= 1:
                        pe.wait_ge(gate_done, (c - 1).count(8, j + 5))
                    f = GATE_ORDER[j] * P
                    for k in range(KD):
                        ins = three_passes(mm_ps[:, j % 4], (wg_hi, wg_lo), (slice(None), k, slice(f, f + P)),
                                           (xt_hi, xt_lo), (slice(None), k), k == 0, k == KD - 1)
                    ins.then_inc(pre_done, 1)

            def shifted_bias():
                pe.wait_ge(w1_step, KD)
                for j in range(KF):
                    for k in range(KD):
                        ins = pe.matmul(z_ps[:, 0, 0, j:j + 1], w1_f[:, k, j * P:(j + 1) * P],
                                        col[:, COL_BETA + k:COL_BETA + k + 1], start=(k == 0), stop=(k == KD - 1))
                ins.then_inc(beta_w1, 1)

            def fc1(c):
                if c.reg is None and c.at == 0:
                    pe.wait_ge(w1_step, 4 * KD)
                    pe.wait_ge(w2_step, 3)
                pe.wait_ge(gt_lo_done, c.count(2, 2))
                for j in range(KF):
                    if j >= 4:
                        pe.wait_ge(silu_done, c.count(8, j - 3))
                    elif (c + 2).exists:
                        pe.wait_ge(gate_done, (c + 2).count(8, j + 5))
                    else:
                        pe.wait_ge(silu_done, (c - 1).count(8, j + 5))
                    for k in range(KD):
                        ins = three_passes(mm_ps[:, j % 4], (w1_hi, w1_lo), (slice(None), k, slice(j * P, j * P + P)),
                                           (gt_hi, gt_lo), (slice(None), k), k == 0, k == KD - 1)
                    ins.then_inc(fc1_done, 1)

            def fc2(c, n):
                u = n // 2
                if n % 2 == 0:
                    if c.at >= 1:
                        pe.wait_ge(final_done, (c - 1).count(2, u + 1))
                    else:
                        pe.wait_ge(b1_ready, 1)
                for k in range(KF):
                    if n == 0:
                        pe.wait_ge(y_lo_done, c.count(8, k + 1))
                    ins = three_passes(z_ps[:, u, n % 2], (y_hi, y_lo), (slice(None), k, slice(n * P, n * P + P)),
                                       (w2_hi, w2_lo), (slice(None), k), k == 0, k == KF - 1)
                if n % 2:
                    ins.then_inc(fc2_done, 1)

            def slot(t):
                ffn, mixed, nxt = t - 2, t - 1, t + 1
                if t.exists:
                    gate_products(t, range(0, 7))
                if ffn.exists:
                    g_turned(ffn)
                if t.exists:
                    gate_products(t, range(7, GJ))
                if ffn.exists:
                    fc1(ffn)
                if mixed.exists and early_h(t):
                    h_turned(mixed)
                if ffn.exists:
                    fc2(ffn, 0)
                    fc2(ffn, 1)
                if nxt.exists:
                    x_turned(nxt)
                if ffn.exists:
                    fc2(ffn, 2)
                if t.reg is None and t.at == 1:
                    shifted_bias()
                if mixed.exists and not early_h(t):
                    h_turned(mixed)
                if ffn.exists:
                    fc2(ffn, 3)

            pe.wait_ge(ident_ready, 2)
            x_turned(Chunk(0))
            pe.wait_ge(wg_split_hi, KD)
            pe.wait_ge(wg_split_lo, KD)

            run_slots(pe, slot)

        @block.scalar
        def _(act):
            act.dma_start(col[:], cols).then_inc(col_in, 16)
            act.dma_start(scale_bc[:], scale_row.partition_broadcast(P)).then_inc(row_in, 16)
            act.dma_start(b2_bc[:], b2_row.partition_broadcast(P)).then_inc(row_in, 16)

            def high_of(c, hi, ready, done):
                for k in range(KD):
                    act.wait_ge(ready, c.count(2, k + 1))
                    act.activation(hi[:, k], t_ps[:, k], ACT.Copy).then_inc(done, 1)

            def gates(c, tiles):
                s = c.seq
                if c.at >= 2 and 0 in tiles:
                    act.wait_ge(h_done, (c - 2).count(3, 3))
                for j in tiles:
                    act.wait_ge(pre_done, c.count(8, j + 1))
                    bias, tile = gate_bias[:, j:j + 1], mm_ps[:, j % 4]
                    if j in I_TILES:
                        ins = act.activation(rec[s][:, 1, j], tile, ACT.Tanh, bias=bias, scale=1.0 / CAP)
                    elif j in F_TILES:
                        ins = act.activation(f_gate[:, s, j - 2], tile, ACT.Sigmoid, bias=bias, scale=-1.0)
                    elif j in Z_TILES:
                        ins = act.activation(rec[s][:, 2, j - 4], tile, ACT.Tanh, bias=bias)
                    else:
                        ins = act.activation(o_gate[:, s, j - 6], tile, ACT.Sigmoid, bias=bias)
                    ins.then_inc(gate_done, 1)

            def exp_i(c):
                act.wait_ge(gate_done, c.count(8, 2))
                act.activation(rec[c.seq][:, 1], rec[c.seq][:, 1], ACT.Exp, scale=CAP).then_inc(i_ready, 1)

            def reciprocal(c):
                r = rec[c.seq][:, 1]
                act.wait_ge(denom_ready, c.count(1, 1))
                act.activation(r, rec[c.seq][:, 0], ACT.Ln).then_inc(recip_done, 1)
                act.wait_ge(recip_done, c.count(2, 1))
                act.activation(r, r, ACT.Exp, scale=-1.0).then_inc(recip_done, 1)

            def square_sums(c):
                if c.at >= 1:
                    act.wait_ge(gt_ready, (c - 1).count(2, 2))
                for n in range(TT):
                    if n % 2 == 0:
                        act.wait_ge(ht_ready, c.count(2, n // 2 + 1))
                    act.activation(g[:, n], t_ps[:, n // 2, n % 2 * D:n % 2 * D + D], ACT.Square,
                                   accum_out=sumsq[:, c.seq, n:n + 1]).then_inc(sq_done, 1)

            def silu(c):
                for j in range(KF):
                    act.wait_ge(fc1_done, c.count(8, j + 1))
                    if c.at >= 1 or j >= 3:
                        act.wait_ge(y_lo_done, c.count(8, j - 2))
                    act.activation(y[:, j % 3], mm_ps[:, j % 4], ACT.Silu, bias=b1_all[:, j:j + 1]
                                   ).then_inc(silu_done, 1)
                    act.wait_ge(silu_done, c.count(8, j + 1))
                    act.activation(y_hi[:, j], y[:, j % 3], ACT.Copy).then_inc(y_hi_done, 1)

            def slot(t):
                ffn, mixed, nxt = t - 2, t - 1, t + 1
                if t.exists:
                    act.preload_act_table_set("sigmoid_and_others")
                    gates(t, range(0, 7))
                if ffn.exists:
                    high_of(ffn, gt_hi, gt_ready, gt_hi_done)
                if t.exists:
                    gates(t, range(7, GJ))
                if early_h(t):
                    act.preload_act_table_set("natural_log_exp_and_others")
                    if mixed.exists:
                        reciprocal(mixed)
                    if t.exists:
                        exp_i(t)
                if ffn.exists:
                    if ffn.reg is None and ffn.at == 0:
                        act.wait_ge(b1_ready, 1)
                    act.preload_act_table_set("silu_and_others")
                    silu(ffn)
                if not early_h(t):
                    act.preload_act_table_set("natural_log_exp_and_others")
                    if mixed.exists:
                        reciprocal(mixed)
                    exp_i(t)
                if nxt.exists:
                    high_of(nxt, xt_hi, xt_ready, xt_hi_done)
                if mixed.exists:
                    square_sums(mixed)

            for k in range(KD):
                act.wait_ge(wg_in, 16 * KD)
                act.activation(wg_hi[:, k], wg_raw[:, k], ACT.Copy).then_inc(wg_split_hi, 1)
            high_of(Chunk(0), xt_hi, xt_ready, xt_hi_done)
            act.wait_ge(bias_ready, 3)
            run_slots(act, slot)

        @block.vector
        def _(dve):
            def stats(c, src, bn, mv, done, per):
                for n in range(TT):
                    dve.bn_stats(bn[:, n], src[:, n]).then_inc(done, 1)
                wait_apart(dve, done, c.count(per, TT), dve_passed)
                for n in range(TT):
                    dve.bn_aggr(mv[:, n], bn[:, n]).then_inc(done, 1)
                dve.wait_ge(done, c.count(per, 2 * TT))

            def ln1(c):
                s = c.seq
                dve.wait_ge(x_landed[s], c.of_seq(16))
                stats(c, x_in[:, s], bn1, mv1, ln1_stat, 10)
                if c.at >= 2:
                    dve.wait_ge(ln1_norm, (c - 2).count(6, 2))
                dve.tensor_scalar(ve1[:, s], mv1[:, :, 1], EPS_LN, None, ALU.add).then_inc(ln1_stat, 1)
                dve.tensor_scalar(nm1[:, s], mv1[:, :, 0], -1.0, None, ALU.mult).then_inc(ln1_stat, 1)

            def low_of(c, hi, lo, hi_done, done):
                for k in range(KD):
                    dve.wait_ge(hi_done, c.count(2, k + 1))
                    dve.tensor_tensor(lo[:, k], t_ps[:, k], hi[:, k].bitcast(F32), ALU.subtract).then_inc(done, 1)

            def scans(c):
                s = c.seq
                r, fg = rec[s], f_gate[:, s]
                dve.wait_ge(i_ready, c.count(1, 1))
                if c.at >= 2:
                    dve.wait_ge(ht_ready, (c - 2).count(2, 2))
                    dve.wait_ge(scan_done, (c - 2).count(7, 7))
                else:
                    dve.wait_ge(carry_zeroed, 2)
                dve.wait_ge(gate_done, c.count(8, 4))
                for k in range(KD):
                    dve.tensor_tensor_scan(r[:, 0, k], fg[:, k], r[:, 1, k], carry[:, s, 0, k:k + 1],
                                           ALU.mult, ALU.max).then_inc(scan_done, 1)
                dve.wait_ge(iz_ready, c.count(1, 1))
                for k in range(KD):
                    dve.tensor_tensor_scan(r[:, 1, k], fg[:, k], r[:, 1, k], carry[:, s, 1, k:k + 1],
                                           ALU.mult, ALU.add).then_inc(scan_done, 1)
                for k in range(KD):
                    dve.tensor_tensor_scan(r[:, 2, k], fg[:, k], r[:, 2, k], carry[:, s, 2, k:k + 1],
                                           ALU.mult, ALU.add).then_inc(scan_done, 1)
                dve.wait_ge(scan_done, c.count(7, 6))
                dve.tensor_copy(carry[:, s], r[:, :, :, T - 1]).then_inc(scan_done, 1)
                dve.wait_ge(scan_done, c.count(7, 7))
                dve.scalar_tensor_tensor(out=r[:, 0], in0=r[:, 0], scalar=EPS_N, in1=r[:, 1],
                                         op0=ALU.mult, op1=ALU.add).then_inc(denom_ready, 1)

            def h(c):
                d, r, oc = (rec[c.seq][:, n] for n in range(3))
                dve.wait_ge(recip_done, c.count(2, 2))
                dve.tensor_tensor(d, d, r, ALU.mult).then_inc(h_done, 1)
                dve.wait_ge(h_done, c.count(3, 1))
                dve.scalar_tensor_tensor(out=d, in0=d, scalar=2.0, in1=r, op0=ALU.subtract, op1=ALU.mult,
                                         reverse0=True).then_inc(h_done, 1)
                dve.wait_ge(oc_ready, c.count(1, 1))
                dve.wait_ge(h_done, c.count(3, 2))
                dve.tensor_tensor(d, d, oc, ALU.mult).then_inc(h_done, 1)

            def mean_square(c):
                dve.wait_ge(sq_done, c.count(4, 4))
                dve.tensor_scalar(meansq[:, c.seq], sumsq[:, c.seq], 1.0 / D, EPS_RMS, ALU.mult, ALU.add
                                  ).then_inc(ms_ready, 1)

            def residual(c):
                s = c.seq
                dve.wait_ge(rrms_ready, c.count(1, 1))
                for n in range(TT):
                    dve.scalar_tensor_tensor(out=g[:, n], in0=t_ps[:, n // 2, n % 2 * D:n % 2 * D + D],
                                             scalar=rrms[:, s, n:n + 1], in1=scale_bc[:],
                                             op0=ALU.mult, op1=ALU.mult).then_inc(hs_done, 1)
                dve.wait_ge(hs_done, c.count(4, 4))
                dve.wait_ge(res_landed[s], c.of_seq(16))
                dve.tensor_tensor(base[:, s], base[:, s], g[:], ALU.add).then_inc(x1_done, 1)
                dve.wait_ge(x1_done, c.count(1, 1))
                stats(c, base[:, s], bn2, mv2, ln2_stat, 11)
                dve.tensor_scalar(ve2[:, s, 0], mv2[:, :, 1], EPS_LN, None, ALU.add).then_inc(ln2_stat, 1)
                dve.tensor_scalar(ve2[:, s, 1], mv2[:, :, 1], 1.0 + EPS_LN, EPS_LN * EPS_LN, ALU.mult, ALU.add
                                  ).then_inc(ln2_stat, 1)
                dve.tensor_scalar(nm2[:, s], mv2[:, :, 0], -1.0, None, ALU.mult).then_inc(ln2_stat, 1)

            def y_low(c):
                for j in range(KF):
                    dve.wait_ge(y_hi_done, c.count(8, j + 1))
                    dve.tensor_tensor(y_lo[:, j], y[:, j % 3], y_hi[:, j].bitcast(F32), ALU.subtract
                                      ).then_inc(y_lo_done, 1)

            def final(c, u):
                dve.wait_ge(fc2_done, c.count(2, u + 1))
                dve.wait_ge(ln2_norm, c.count(13, 13))
                if c.at >= 1:
                    dve.wait_ge(out_landed[u], c.count(16, 0))
                dve.scalar_tensor_tensor(out=out_sb[:, u], in0=z_ps[:, u], scalar=0.5,
                                         in1=base[:, c.seq, 2 * u:2 * u + 2],
                                         op0=ALU.mult, op1=ALU.add).then_inc(final_done, 1)

            def dequantise():
                dve.wait_ge(q1_in, 16)
                dve.wait_ge(s1_in, 16)
                for k in range(KD):
                    dve.scalar_tensor_tensor(out=w1_f[:, k], in0=q1[:, k], scalar=-ZERO_POINT, in1=s1[:, k],
                                             op0=ALU.add, op1=ALU.mult).then_inc(w1_step, 1)
                dve.wait_ge(q2_in, 16)
                dve.wait_ge(s2_in, 16)
                dve.scalar_tensor_tensor(out=w2_f, in0=q2[:], scalar=-ZERO_POINT, in1=s2,
                                         op0=ALU.add, op1=ALU.mult).then_inc(w2_step, 1)
                dve.wait_ge(w2_step, 1)
                dve.tensor_copy(w2_hi[:], w2_f).then_inc(w2_step, 1)
                dve.wait_ge(w2_step, 2)
                dve.tensor_tensor(w2_lo[:], w2_f, w2_hi[:].bitcast(F32), ALU.subtract).then_inc(w2_step, 1)
                dve.wait_ge(w1_step, KD)
                for k in range(KD):
                    dve.tensor_scalar(s1[:, k], w1_f[:, k], col[:, COL_GAMMA + k:COL_GAMMA + k + 1], None, ALU.mult
                                      ).then_inc(w1_step, 1)
                dve.wait_ge(w1_step, 2 * KD)
                for k in range(KD):
                    dve.tensor_copy(w1_hi[:, k], s1[:, k]).then_inc(w1_step, 1)
                dve.wait_ge(w1_step, 3 * KD)
                for k in range(KD):
                    dve.tensor_tensor(w1_lo[:, k], s1[:, k], w1_hi[:, k].bitcast(F32), ALU.subtract
                                      ).then_inc(w1_step, 1)

            def slot(t):
                ffn, mixed, nxt = t - 2, t - 1, t + 1
                if t.reg is None and t.at == 2:
                    dve.wait_ge(beta_w1, 1)
                    dve.tensor_tensor(b1_all[:], z_ps[:, 0, 0, 0:KF], col[:, COL_B1:COL_B1 + KF], ALU.add
                                      ).then_inc(b1_ready, 1)
                if ffn.exists:
                    low_of(ffn, gt_hi, gt_lo, gt_hi_done, gt_lo_done)
                if mixed.exists and not early_h(mixed):
                    scans(mixed)
                if nxt.exists:
                    ln1(nxt)
                if t.reg is None and t.at == 0:
                    dequantise()
                if mixed.exists and early_h(t):
                    h(mixed)
                if ffn.exists:
                    y_low(ffn)
                if mixed.exists and not early_h(t):
                    h(mixed)
                if early_h(t):
                    if mixed.exists:
                        mean_square(mixed)
                        residual(mixed)
                if ffn.exists:
                    final(ffn, 0)
                if nxt.exists:
                    low_of(nxt, xt_hi, xt_lo, xt_hi_done, xt_lo_done)
                if mixed.exists and not early_h(t):
                    mean_square(mixed)
                    residual(mixed)
                if ffn.exists:
                    final(ffn, 1)
                if t.exists and early_h(t):
                    scans(t)

            dve.memset(minus_half[:], -0.5).then_inc(half_ready, 1)
            dve.memset(carry[:, :, 0], 1.0).then_inc(carry_zeroed, 1)
            dve.memset(carry[:, :, 1:3], 0.0).then_inc(carry_zeroed, 1)
            ln1(Chunk(0))
            dve.wait_ge(col_in, 16)
            dve.scalar_tensor_tensor(out=gate_bias[:, 0:2], in0=col[:, 0:2], scalar=1.0,
                                     in1=col[:, COL_IB:COL_IB + KD], op0=ALU.mult, op1=ALU.add).then_inc(bias_ready, 1)
            dve.tensor_scalar(gate_bias[:, 2:4], col[:, 2:4], -1.0, None, ALU.mult)
            dve.tensor_copy(gate_bias[:, 4:6], col[:, 6:8])
            dve.tensor_copy(gate_bias[:, 6:8], col[:, 4:6]).then_inc(bias_ready, 1)
            dve.wait_ge(bias_ready, 2)
            dve.tensor_scalar(gate_bias[:, 0:2], gate_bias[:, 0:2], 1.0 / CAP, None, ALU.mult).then_inc(bias_ready, 1)
            for k in range(KD):
                dve.wait_ge(wg_split_hi, k + 1)
                dve.tensor_tensor(wg_lo[:, k], wg_raw[:, k], wg_hi[:, k].bitcast(F32), ALU.subtract
                                  ).then_inc(wg_split_lo, 1)
            low_of(Chunk(0), xt_hi, xt_lo, xt_hi_done, xt_lo_done)
            dve.wait_ge(row_in, 32)
            run_slots(dve, slot)

        @block.gpsimd
        def _(pool):
            def normalise(dst, src, mul, add, done):
                for n in range(TT):
                    pool.tensor_scalar(dst[:, n], src[:, n], mul[:, n:n + 1], add[:, n:n + 1], ALU.mult, ALU.add
                                       ).then_inc(done, 1)

            def ln1(c):
                s = c.seq
                pool.wait_ge(ln1_stat, c.count(10, 10))
                pool.tensor_tensor(r1[:], ve1[:, s], minus_half[:, 0:TT], ALU.pow).then_inc(ln1_norm, 1)
                pool.wait_ge(ln1_norm, c.count(6, 1))
                pool.tensor_tensor(nr1[:], nm1[:, s], r1[:], ALU.mult).then_inc(ln1_norm, 1)
                wait_apart(pool, ln1_norm, c.count(6, 2), pool_passed)
                if c.at >= 1:
                    wait_apart(pool, xt_ready, (c - 1).count(2, 2), pool_passed)
                normalise(xn, x_in[:, s], r1, nr1, ln1_norm)

            def input_times_z(c):
                r = rec[c.seq]
                pool.wait_ge(i_ready, c.count(1, 1))
                pool.wait_ge(gate_done, c.count(8, 6))
                pool.tensor_tensor(r[:, 2], r[:, 2], r[:, 1], ALU.mult).then_inc(iz_ready, 1)

            def o_times_c(c):
                oc = rec[c.seq][:, 2]
                pool.wait_ge(scan_done, c.count(7, 7))
                pool.wait_ge(gate_done, c.count(8, 8))
                pool.tensor_tensor(oc, oc, o_gate[:, c.seq], ALU.mult).then_inc(oc_ready, 1)

            def rrms_of(c):
                pool.wait_ge(ms_ready, c.count(1, 1))
                pool.tensor_tensor(rrms[:, c.seq], meansq[:, c.seq], minus_half[:, 0:TT], ALU.pow
                                   ).then_inc(rrms_ready, 1)

            def ln2(c):
                s = c.seq
                pool.wait_ge(ln2_stat, c.count(11, 11))
                pool.tensor_tensor(r2[:].rearrange("p a t -> p (a t)"), ve2[:, s].rearrange("p a t -> p (a t)"),
                                   minus_half[:], ALU.pow).then_inc(ln2_norm, 1)
                pool.wait_ge(ln2_norm, c.count(13, 1))
                pool.tensor_tensor(nr2[:, 0], nm2[:, s], r2[:, 0], ALU.mult).then_inc(ln2_norm, 1)
                pool.tensor_tensor(nr2[:, 1], nm2[:, s], r2[:, 1], ALU.mult).then_inc(ln2_norm, 1)
                pool.tensor_scalar(up2[:], r2[:, 0], 1.0, None, ALU.add).then_inc(ln2_norm, 1)
                wait_apart(pool, ln2_norm, c.count(13, 4), pool_passed)
                normalise(g, base[:, s], r2[:, 1], nr2[:, 1], ln2_norm)
                wait_apart(pool, ln2_norm, c.count(13, 8), pool_passed)
                normalise(base[:, s], base[:, s], up2, nr2[:, 0], ln2_norm)
                pool.wait_ge(ln2_norm, c.count(13, 12))
                pool.tensor_tensor(base[:, s], base[:, s], b2_bc[:].unsqueeze(1).to_broadcast([P, TT, D]), ALU.add
                                   ).then_inc(ln2_norm, 1)

            def slot(t):
                mixed, nxt = t - 1, t + 1
                if nxt.exists:
                    ln1(nxt)
                if mixed.exists:
                    o_times_c(mixed)
                if t.exists:
                    input_times_z(t)
                if mixed.exists:
                    rrms_of(mixed)
                    ln2(mixed)

            pool.memset(ident[:], 0.0).then_inc(ident_ready, 1)
            pool.wait_ge(ident_ready, 1)
            pool.affine_select(out=ident[:], in_=ident[:], compare_op=ALU.not_equal, fill=1.0, base=0,
                               pattern=[[-1, P]], channel_multiplier=1).then_inc(ident_ready, 1)
            pool.wait_ge(half_ready, 1)
            ln1(Chunk(0))
            pool.wait_ge(row_in, 32)
            pool.tensor_scalar(b2_bc[:], b2_bc[:], 0.5, 0.0, ALU.mult, ALU.add).then_inc(half_ready, 1)
            pool.wait_ge(half_ready, 2)
            run_slots(pool, slot)


def kernel(L0_attn_x, L0_attn_W, L0_attn_b, L0_attn_input_bias, L0_attn_scale, L0_ffn_ln_gamma, L0_ffn_ln_beta,
           L0_ffn_fc1_q, L0_ffn_fc1_scales, L0_ffn_fc1_bias, L0_ffn_fc2_q, L0_ffn_fc2_scales, L0_ffn_fc2_bias):
    import numpy as np
    import concourse.bacc as bacc
    from concourse.bass_utils import run_bass_kernel_spmd

    def by_partition(v):
        return np.asarray(v).reshape(-1, P).T

    arrays = {
        "x": np.asarray(L0_attn_x),
        "w_gates": np.asarray(L0_attn_W),
        "cols": np.ascontiguousarray(np.concatenate([by_partition(v) for v in (
            L0_attn_b, L0_attn_input_bias, L0_ffn_ln_gamma, L0_ffn_ln_beta, L0_ffn_fc1_bias)], axis=1)),
        "scale_row": np.asarray(L0_attn_scale),
        "fc1_q": np.asarray(L0_ffn_fc1_q),
        "fc1_scales": np.asarray(L0_ffn_fc1_scales),
        "fc2_q": np.asarray(L0_ffn_fc2_q),
        "fc2_scales": np.asarray(L0_ffn_fc2_scales),
        "b2_row": np.asarray(L0_ffn_fc2_bias),
    }
    nc = bacc.Bacc("TRN2", target_bir_lowering=False, num_devices=1)
    args = [nc.dram_tensor(n, a.shape, mybir.dt.from_np(a.dtype), kind="ExternalInput").ap() for n, a in arrays.items()]
    out = nc.dram_tensor("out", (SEQS, STEPS, D), F32, kind="ExternalOutput").ap()
    layer(nc, *args, out)
    r = run_bass_kernel_spmd(nc, [arrays], core_ids=[0])
    return r.results[0]["out"]
```

```python
from contextlib import ExitStack

import concourse.bass as bass
from concourse import mybir

F32 = mybir.dt.float32
F32R = mybir.dt.float32r
I32 = mybir.dt.int32
ALU = mybir.AluOpType
ACT = mybir.ActivationFunctionType

P = 128
SEQS, STEPS, D = 2, 2048, 256
GATES, F = 4 * D, 1024
T = 512
TT = T // P
CHUNKS = SEQS * STEPS // T
KD = D // P
KF = F // P
GJ = GATES // P
CAP = 10.0
EPS_N, EPS_RMS, EPS_LN = 1e-6, 1e-8, 1e-5
ZERO_POINT = 128.0
GATE_ORDER = [0, 1, 2, 3, 6, 7, 4, 5]
I_TILES, F_TILES, Z_TILES, O_TILES = (0, 1), (2, 3), (4, 5), (6, 7)
COL_B, COL_IB, COL_GAMMA, COL_BETA, COL_B1 = 0, GJ, GJ + KD, GJ + 2 * KD, GJ + 3 * KD
COLS = COL_B1 + KF
LOOP_FROM, LOOP_TO = 3, 7
LAST_SLOT = CHUNKS + 1


class Chunk:

    def __init__(self, at, reg=None):
        self.at, self.reg = at, reg

    def __add__(self, n):
        return Chunk(self.at + n, self.reg)

    def __sub__(self, n):
        return self + -n

    @property
    def exists(self):
        return 0 <= self.at < CHUNKS

    @property
    def seq(self):
        return self.at % SEQS

    def block(self):
        return self.at // SEQS if self.reg is None else self.reg + self.at // SEQS

    def count(self, per, k):
        n = per * self.at + k
        return n if self.reg is None else self.reg * (2 * per) + n

    def of_seq(self, per):
        n = per * (self.at // SEQS + 1)
        return n if self.reg is None else self.reg * per + n


def run_slots(eng, slot):
    for t in range(LOOP_FROM):
        slot(Chunk(t))
    with eng.Fori(0, (LOOP_TO - LOOP_FROM) // 2) as i:
        slot(Chunk(LOOP_FROM, i))
        slot(Chunk(LOOP_FROM + 1, i))
    for t in range(LOOP_TO, LAST_SLOT + 1):
        slot(Chunk(t))


def is_slot(t, n):
    return t.reg is None and t.at == n


def early_h(t):
    return t.reg is None and t.at >= CHUNKS - 1


def wait_apart(eng, semaphore, n, passed):
    eng.wait_ge(semaphore, n)
    eng.sem_inc(passed, 1)


def layer(nc, x, w_gates, cols, scale_row, fc1_q, fc1_scales, fc2_q, fc2_scales, b2_row, out):
    x_view = x.rearrange("s (c t p) d -> s c p t d", t=TT, p=P)
    out_view = out.rearrange("s (c t p) d -> s c p t d", t=TT, p=P)

    with ExitStack() as ctx:
        def sb(name, shape, dt=F32):
            return ctx.enter_context(nc.sbuf_tensor(name, shape, dt))

        def ps(name, shape):
            return ctx.enter_context(nc.psum_tensor(name, shape, F32))

        def sem(name):
            return ctx.enter_context(nc.semaphore(name))

        wg_hi = sb("wg_hi", [P, KD, GATES], F32R)
        wg_lo = sb("wg_lo", [P, KD, GATES], F32R)
        w1_hi = sb("w1_hi", [P, KD, F], F32R)
        w1_lo = sb("w1_lo", [P, KD, F], F32R)
        w2_hi = sb("w2_hi", [P, KF, D], F32R)
        w2_lo = sb("w2_lo", [P, KF, D], F32R)
        wg_raw = sb("wg_raw", [P, KD, GATES])
        q1 = sb("q1", [P, KD, F], I32)
        q2 = sb("q2", [P, KF, D], I32)
        s1 = sb("s1", [P, KD, F])
        s2 = wg_raw[:].rearrange("p k (h d) -> p (k h) d", d=D)
        w1_f = q1[:].bitcast(F32)
        w2_f = q2[:].bitcast(F32)
        ident = sb("ident", [P, P])
        col = sb("col", [P, COLS])
        gate_bias = sb("gate_bias", [P, GJ])
        b1_all = sb("b1_all", [P, KF])
        scale_bc = sb("scale_bc", [P, D])
        b2_bc = sb("b2_bc", [P, D])
        x_in = sb("x_in", [P, 2, TT, D])
        xn = sb("xn", [P, TT, D])
        g = sb("g", [P, TT, D])
        base = sb("base", [P, 2, TT, D])
        out_sb = sb("out_sb", [P, 2, 2, D])
        xt_hi = sb("xt_hi", [P, KD, T], F32R)
        xt_lo = sb("xt_lo", [P, KD, T], F32R)
        gt_hi = sb("gt_hi", [P, KD, T], F32R)
        gt_lo = sb("gt_lo", [P, KD, T], F32R)
        y = sb("y", [P, 3, T])
        y_hi = sb("y_hi", [P, KF, T], F32R)
        y_lo = sb("y_lo", [P, KF, T], F32R)
        rec = [sb(f"rec{s}", [P, 3, KD, T]) for s in range(2)]
        f_gate = sb("f_gate", [P, 2, KD, T])
        o_gate = sb("o_gate", [P, 2, KD, T])
        carry = sb("carry", [P, 2, 3, KD])
        bn1 = sb("bn1", [P, TT, 6])
        mv1 = sb("mv1", [P, TT, 2])
        ve1 = sb("ve1", [P, 2, TT])
        nm1 = sb("nm1", [P, 2, TT])
        r1 = sb("r1", [P, TT])
        nr1 = sb("nr1", [P, TT])
        bn2 = sb("bn2", [P, TT, 6])
        mv2 = sb("mv2", [P, TT, 2])
        ve2 = sb("ve2", [P, 2, 2, TT])
        nm2 = sb("nm2", [P, 2, TT])
        r2 = sb("r2", [P, 2, TT])
        nr2 = sb("nr2", [P, 2, TT])
        up2 = sb("up2", [P, TT])
        sumsq = sb("sumsq", [P, 2, TT])
        meansq = sb("meansq", [P, 2, TT])
        rrms = sb("rrms", [P, 2, TT])
        minus_half = sb("minus_half", [P, TT])

        mm_ps = ps("mm_ps", [P, 4, T])
        z_ps = ps("z_ps", [P, 2, 2, D])
        t_ps = ps("t_ps", [P, 2, T])

        ident_ready = sem("ident_ready")
        half_ready = sem("half_ready")
        wg_in, q1_in, q2_in, s1_in, col_in, row_in = (sem(n) for n in (
            "wg_in", "q1_in", "q2_in", "s1_in", "col_in", "row_in"))
        s2_in = sem("s2_in")
        bias_ready = sem("bias_ready")
        carry_zeroed = sem("carry_zeroed")
        wg_split_hi, wg_split_lo = sem("wg_split_hi"), sem("wg_split_lo")
        w1_shifted, w1_scaled, w1_gamma, w1_rounded, w1_ready = (sem(n) for n in (
            "w1_shifted", "w1_scaled", "w1_gamma", "w1_rounded", "w1_ready"))
        w2_shifted, w2_scaled, w2_rounded, w2_ready = (sem(n) for n in (
            "w2_shifted", "w2_scaled", "w2_rounded", "w2_ready"))
        beta_w1 = sem("beta_w1")
        b1_ready = sem("b1_ready")
        x_landed = [sem(f"x_landed{s}") for s in range(2)]
        res_landed = [sem(f"res_landed{s}") for s in range(2)]
        out_landed = [sem(f"out_landed{u}") for u in range(2)]
        ln1_stat = sem("ln1_stat")
        ln1_norm = sem("ln1_norm")
        xt_ready = sem("xt_ready")
        xt_hi_done = sem("xt_hi_done")
        xt_lo_done = sem("xt_lo_done")
        pre_done = sem("pre_done")
        gate_done = sem("gate_done")
        i_ready = sem("i_ready")
        iz_ready = sem("iz_ready")
        scan_done = sem("scan_done")
        denom_ready = sem("denom_ready")
        recip_done = sem("recip_done")
        oc_ready = sem("oc_ready")
        h_done = sem("h_done")
        ht_ready = sem("ht_ready")
        sq_done = sem("sq_done")
        ms_ready = sem("ms_ready")
        rrms_ready = sem("rrms_ready")
        hs_done = sem("hs_done")
        x1_done = sem("x1_done")
        ln2_stat = sem("ln2_stat")
        ln2_norm = sem("ln2_norm")
        gt_ready = sem("gt_ready")
        gt_hi_done = sem("gt_hi_done")
        gt_lo_done = sem("gt_lo_done")
        fc1_done = sem("fc1_done")
        silu_done = sem("silu_done")
        y_even_hi = sem("y_even_hi")
        y_odd_hi = sem("y_odd_hi")
        y_lo_done = sem("y_lo_done")
        fc2_done = sem("fc2_done")
        final_done = sem("final_done")

        sp_passed, dve_passed, pool_passed = sem("sp_passed"), sem("dve_passed"), sem("pool_passed")

        block = ctx.enter_context(nc.Block())

        @block.sync
        def _(sp):
            def load_x(c):
                if c.at >= 2:
                    wait_apart(sp, ln1_norm, (c - 2).count(6, 6), sp_passed)
                sp.dma_start(x_in[:, c.seq], x_view[c.seq, bass.ds(c.block(), 1)].rearrange("c p t d -> (c p) t d")
                             ).then_inc(x_landed[c.seq], 16)

            sp.dma_start(x_in[:, 0], x_view[0, 0]).then_inc(x_landed[0], 16)
            for k in range(KD):
                sp.dma_start(wg_raw[:, k], w_gates[k * P:(k + 1) * P, :]).then_inc(wg_in, 16)
            sp.dma_start(x_in[:, 1], x_view[1, 0]).then_inc(x_landed[1], 16)
            sp.dma_start(q1[:], fc1_q.rearrange("(k p) f -> p k f", p=P)).then_inc(q1_in, 16)
            sp.dma_start(s1[:], fc1_scales.partition_broadcast(P)).then_inc(s1_in, 16)
            sp.dma_start(q2[:], fc2_q.rearrange("(k p) f -> p k f", p=P)).then_inc(q2_in, 16)
            sp.wait_ge(wg_split_lo, KD)
            sp.dma_start(s2, fc2_scales.partition_broadcast(P)).then_inc(s2_in, 16)

            def slot(t):
                if (t + 1).exists and not (t.reg is None and t.at == 0):
                    load_x(t + 1)
                c = t - 2
                if c.exists:
                    for u in range(2):
                        wait_apart(sp, final_done, c.count(2, u + 1), sp_passed)
                        sp.dma_start(
                            out_view[c.seq, bass.ds(c.block(), 1), :, 2 * u:2 * u + 2].rearrange("c p t d -> (c p) t d"),
                            out_sb[:, u]).then_inc(out_landed[u], 16)
                if t.exists:
                    sp.dma_start(base[:, t.seq], x_view[t.seq, bass.ds(t.block(), 1)].rearrange("c p t d -> (c p) t d")
                                 ).then_inc(res_landed[t.seq], 16)

            run_slots(sp, slot)
            for u in range(2):
                sp.wait_ge(out_landed[u], 16 * CHUNKS)

        @block.tensor
        def _(pe):
            def three_passes(dst, w_pair, w_at, a_pair, a_at, first, last):
                (wh, wl), (ah, al) = w_pair, a_pair
                pe.matmul(dst, wh[w_at], ah[a_at], start=first, stop=False)
                pe.matmul(dst, wh[w_at], al[a_at], start=False, stop=False)
                return pe.matmul(dst, wl[w_at], ah[a_at], start=False, stop=last)

            def turn_back(src, ready):
                for k in range(KD):
                    yield k
                    for n in range(TT):
                        ins = pe.transpose(t_ps[:, k, n * P:(n + 1) * P], src[:, n, k * P:(k + 1) * P], ident[:])
                    ins.then_inc(ready, 1)

            def x_turned(c):
                pe.wait_ge(ln1_norm, c.count(6, 6))
                for k in turn_back(xn, xt_ready):
                    if c.at >= 3:
                        pe.wait_ge(gt_lo_done, (c - 3).count(2, k + 1))
                    elif c.at >= 1:
                        pe.wait_ge(xt_lo_done, (c - 1).count(2, k + 1))

            def g_turned(c):
                pe.wait_ge(ln2_norm, c.count(14, 6))
                for k in turn_back(g, gt_ready):
                    pe.wait_ge(hs_done, c.count(4, 2 * k + 2))

            def h_turned(c):
                pe.wait_ge(h_done, c.count(3, 3))
                for u in range(2):
                    if (c + 2).exists:
                        pe.wait_ge(xt_lo_done, (c + 2).count(2, u + 1))
                    else:
                        pe.wait_ge(gt_lo_done, (c - 1).count(2, u + 1))
                    for n in range(2):
                        for k in range(KD):
                            at = (2 * n + k) * P
                            tok = (2 * u + n) * P
                            ins = pe.transpose(t_ps[:, u, at:at + P], rec[c.seq][:, 0, k, tok:tok + P], ident[:])
                    ins.then_inc(ht_ready, 1)

            def gate_products(c, tiles):
                for j in tiles:
                    if j >= 4:
                        pe.wait_ge(gate_done, c.count(8, j - 3))
                    elif c.at >= 3:
                        pe.wait_ge(silu_done, (c - 3).count(8, j + 5))
                    elif c.at >= 1:
                        pe.wait_ge(gate_done, (c - 1).count(8, j + 5))
                    f = GATE_ORDER[j] * P
                    for k in range(KD):
                        if j == 0:
                            pe.wait_ge(xt_lo_done, c.count(2, k + 1))
                        ins = three_passes(mm_ps[:, j % 4], (wg_hi, wg_lo), (slice(None), k, slice(f, f + P)),
                                           (xt_hi, xt_lo), (slice(None), k), k == 0, k == KD - 1)
                    ins.then_inc(pre_done, 1)

            def shifted_bias():
                pe.wait_ge(w1_scaled, 1)
                for j in range(KF):
                    for k in range(KD):
                        ins = pe.matmul(z_ps[:, 0, 0, j:j + 1], w1_f[:, k, j * P:(j + 1) * P],
                                        col[:, COL_BETA + k:COL_BETA + k + 1], start=(k == 0), stop=(k == KD - 1))
                ins.then_inc(beta_w1, 1)

            def fc1(c):
                if c.reg is None and c.at == 0:
                    pe.wait_ge(w1_ready, 1)
                    pe.wait_ge(w2_ready, 1)
                for j in range(KF):
                    if j >= 4:
                        pe.wait_ge(silu_done, c.count(8, j - 3))
                    elif (c + 2).exists:
                        pe.wait_ge(gate_done, (c + 2).count(8, j + 5))
                    else:
                        pe.wait_ge(silu_done, (c - 1).count(8, j + 5))
                    for k in range(KD):
                        if j == 0:
                            pe.wait_ge(gt_lo_done, c.count(2, k + 1))
                        ins = three_passes(mm_ps[:, j % 4], (w1_hi, w1_lo), (slice(None), k, slice(j * P, j * P + P)),
                                           (gt_hi, gt_lo), (slice(None), k), k == 0, k == KD - 1)
                    ins.then_inc(fc1_done, 1)

            def fc2(c, n):
                u = n // 2
                if n % 2 == 0:
                    if c.at >= 1:
                        pe.wait_ge(final_done, (c - 1).count(2, u + 1))
                    else:
                        pe.wait_ge(b1_ready, 1)
                for k in range(KF):
                    if n == 0:
                        pe.wait_ge(y_lo_done, c.count(8, k + 1))
                    ins = three_passes(z_ps[:, u, n % 2], (y_hi, y_lo), (slice(None), k, slice(n * P, n * P + P)),
                                       (w2_hi, w2_lo), (slice(None), k), k == 0, k == KF - 1)
                if n % 2:
                    ins.then_inc(fc2_done, 1)

            def slot(t):
                ffn, mixed, nxt = t - 2, t - 1, t + 1
                if t.exists:
                    gate_products(t, range(0, 7))
                if ffn.exists:
                    g_turned(ffn)
                if t.exists:
                    gate_products(t, range(7, GJ))
                if ffn.exists:
                    fc1(ffn)
                if mixed.exists and early_h(t):
                    h_turned(mixed)
                if ffn.exists:
                    fc2(ffn, 0)
                    fc2(ffn, 1)
                if nxt.exists:
                    x_turned(nxt)
                if ffn.exists:
                    fc2(ffn, 2)
                if mixed.exists and not early_h(t):
                    h_turned(mixed)
                if is_slot(t, 1):
                    shifted_bias()
                if ffn.exists:
                    fc2(ffn, 3)

            pe.wait_ge(ident_ready, 2)
            x_turned(Chunk(0))
            pe.wait_ge(wg_split_hi, KD)
            pe.wait_ge(wg_split_lo, KD)

            run_slots(pe, slot)

        @block.scalar
        def _(act):
            act.dma_start(col[:], cols).then_inc(col_in, 16)
            act.dma_start(scale_bc[:], scale_row.partition_broadcast(P)).then_inc(row_in, 16)
            act.dma_start(b2_bc[:], b2_row.partition_broadcast(P)).then_inc(row_in, 16)

            def high_of(c, hi, ready, done):
                for k in range(KD):
                    act.wait_ge(ready, c.count(2, k + 1))
                    act.activation(hi[:, k], t_ps[:, k], ACT.Copy).then_inc(done, 1)

            def gates(c, tiles):
                s = c.seq
                if c.at >= 2 and 0 in tiles:
                    act.wait_ge(h_done, (c - 2).count(3, 3))
                for j in tiles:
                    act.wait_ge(pre_done, c.count(8, j + 1))
                    bias, tile = gate_bias[:, j:j + 1], mm_ps[:, j % 4]
                    if j in I_TILES:
                        ins = act.activation(rec[s][:, 1, j], tile, ACT.Tanh, bias=bias, scale=1.0 / CAP)
                    elif j in F_TILES:
                        ins = act.activation(f_gate[:, s, j - 2], tile, ACT.Sigmoid, bias=bias, scale=-1.0)
                    elif j in Z_TILES:
                        ins = act.activation(rec[s][:, 2, j - 4], tile, ACT.Tanh, bias=bias)
                    else:
                        ins = act.activation(o_gate[:, s, j - 6], tile, ACT.Sigmoid, bias=bias)
                    ins.then_inc(gate_done, 1)

            def exp_i(c):
                act.wait_ge(gate_done, c.count(8, 2))
                act.activation(rec[c.seq][:, 1], rec[c.seq][:, 1], ACT.Exp, scale=CAP).then_inc(i_ready, 1)

            def reciprocal(c):
                r = rec[c.seq][:, 1]
                act.wait_ge(denom_ready, c.count(1, 1))
                act.activation(r, rec[c.seq][:, 0], ACT.Ln).then_inc(recip_done, 1)
                act.wait_ge(recip_done, c.count(2, 1))
                act.activation(r, r, ACT.Exp, scale=-1.0).then_inc(recip_done, 1)

            def square_sums(c):
                if c.at >= 1:
                    act.wait_ge(gt_ready, (c - 1).count(2, 2))
                for n in range(TT):
                    if n % 2 == 0:
                        act.wait_ge(ht_ready, c.count(2, n // 2 + 1))
                    act.activation(g[:, n], t_ps[:, n // 2, n % 2 * D:n % 2 * D + D], ACT.Square,
                                   accum_out=sumsq[:, c.seq, n:n + 1]).then_inc(sq_done, 1)

            def silu(c):
                for j in range(KF):
                    act.wait_ge(fc1_done, c.count(8, j + 1))
                    if c.at >= 1 or j >= 3:
                        act.wait_ge(y_lo_done, c.count(8, j - 2))
                    act.activation(y[:, j % 3], mm_ps[:, j % 4], ACT.Silu, bias=b1_all[:, j:j + 1]
                                   ).then_inc(silu_done, 1)
                    if j % 2 == 0:
                        act.wait_ge(silu_done, c.count(8, j + 1))
                        act.activation(y_hi[:, j], y[:, j % 3], ACT.Copy).then_inc(y_even_hi, 1)

            def slot(t):
                ffn, mixed, nxt = t - 2, t - 1, t + 1
                if is_slot(t, 0):
                    act.preload_act_table_set("sigmoid_and_others")
                    gates(t, I_TILES)
                    exp_i(t)
                    gates(t, range(2, GJ))
                elif is_slot(t, 1):
                    act.preload_act_table_set("natural_log_exp_and_others")
                    reciprocal(mixed)
                    act.preload_act_table_set("sigmoid_and_others")
                    gates(t, range(GJ))
                else:
                    if t.exists:
                        act.preload_act_table_set("sigmoid_and_others")
                        gates(t, range(0, 7))
                    if ffn.exists:
                        high_of(ffn, gt_hi, gt_ready, gt_hi_done)
                    if t.exists:
                        gates(t, range(7, GJ))
                    if early_h(t):
                        act.preload_act_table_set("natural_log_exp_and_others")
                        if mixed.exists:
                            reciprocal(mixed)
                        if t.exists:
                            exp_i(t)
                    if is_slot(t, 2):
                        act.wait_ge(b1_ready, 1)
                    act.preload_act_table_set("silu_and_others")
                    silu(ffn)
                    if not early_h(t):
                        act.preload_act_table_set("natural_log_exp_and_others")
                        reciprocal(mixed)
                        exp_i(t)
                if nxt.exists:
                    high_of(nxt, xt_hi, xt_ready, xt_hi_done)
                if is_slot(t, 0):
                    scale_and_round_w1()
                if mixed.exists:
                    square_sums(mixed)
                if is_slot(t, 1):
                    act.preload_act_table_set("natural_log_exp_and_others")
                    exp_i(t)
                    round_w2()

            def scale_and_round_w1():
                act.wait_ge(w1_scaled, 1)
                for k in range(KD):
                    act.activation(s1[:, k], w1_f[:, k], ACT.Copy, scale=col[:, COL_GAMMA + k:COL_GAMMA + k + 1]
                                   ).then_inc(w1_gamma, 1)
                act.wait_ge(w1_gamma, KD)
                act.activation(w1_hi[:], s1[:], ACT.Copy).then_inc(w1_rounded, 1)
                act.wait_ge(q2_in, 16)
                act.activation(w2_f, q2[:], ACT.Copy, bias=-ZERO_POINT).then_inc(w2_shifted, 1)

            def round_w2():
                act.wait_ge(w2_scaled, 1)
                act.activation(w2_hi[:], w2_f, ACT.Copy).then_inc(w2_rounded, 1)

            for k in range(KD):
                act.wait_ge(wg_in, 16 * KD)
                act.activation(wg_hi[:, k], wg_raw[:, k], ACT.Copy).then_inc(wg_split_hi, 1)
            high_of(Chunk(0), xt_hi, xt_ready, xt_hi_done)
            act.wait_ge(q1_in, 16)
            act.activation(w1_f, q1[:], ACT.Copy, bias=-ZERO_POINT).then_inc(w1_shifted, 1)
            act.wait_ge(bias_ready, 3)
            run_slots(act, slot)

        @block.vector
        def _(dve):
            def stats(c, src, bn, mv, done, per):
                for n in range(TT):
                    dve.bn_stats(bn[:, n], src[:, n]).then_inc(done, 1)
                wait_apart(dve, done, c.count(per, TT), dve_passed)
                for n in range(TT):
                    dve.bn_aggr(mv[:, n], bn[:, n]).then_inc(done, 1)
                dve.wait_ge(done, c.count(per, 2 * TT))

            def ln1(c):
                s = c.seq
                dve.wait_ge(x_landed[s], c.of_seq(16))
                stats(c, x_in[:, s], bn1, mv1, ln1_stat, 10)
                if c.at >= 2:
                    dve.wait_ge(ln1_norm, (c - 2).count(6, 2))
                dve.tensor_scalar(ve1[:, s], mv1[:, :, 1], EPS_LN, None, ALU.add).then_inc(ln1_stat, 1)
                dve.tensor_scalar(nm1[:, s], mv1[:, :, 0], -1.0, None, ALU.mult).then_inc(ln1_stat, 1)

            def low_of(c, hi, lo, hi_done, done):
                for k in range(KD):
                    dve.wait_ge(hi_done, c.count(2, k + 1))
                    dve.tensor_tensor(lo[:, k], t_ps[:, k], hi[:, k].bitcast(F32), ALU.subtract).then_inc(done, 1)

            def first_scans(c):
                s = c.seq
                r, fg = rec[s], f_gate[:, s]
                dve.wait_ge(i_ready, c.count(1, 1))
                if c.at >= 2:
                    dve.wait_ge(ht_ready, (c - 2).count(2, 2))
                    dve.wait_ge(scan_done, (c - 2).count(7, 7))
                else:
                    dve.wait_ge(carry_zeroed, 2)
                dve.wait_ge(gate_done, c.count(8, 4))
                for k in range(KD):
                    dve.tensor_tensor_scan(r[:, 0, k], fg[:, k], r[:, 1, k], carry[:, s, 0, k:k + 1],
                                           ALU.mult, ALU.max).then_inc(scan_done, 1)
                dve.wait_ge(iz_ready, c.count(1, 1))
                for k in range(KD):
                    dve.tensor_tensor_scan(r[:, 1, k], fg[:, k], r[:, 1, k], carry[:, s, 1, k:k + 1],
                                           ALU.mult, ALU.add).then_inc(scan_done, 1)

            def last_scans(c):
                s = c.seq
                r, fg = rec[s], f_gate[:, s]
                for k in range(KD):
                    dve.tensor_tensor_scan(r[:, 2, k], fg[:, k], r[:, 2, k], carry[:, s, 2, k:k + 1],
                                           ALU.mult, ALU.add).then_inc(scan_done, 1)
                dve.wait_ge(scan_done, c.count(7, 6))
                dve.tensor_copy(carry[:, s], r[:, :, :, T - 1]).then_inc(scan_done, 1)
                dve.wait_ge(scan_done, c.count(7, 7))
                dve.scalar_tensor_tensor(out=r[:, 0], in0=r[:, 0], scalar=EPS_N, in1=r[:, 1],
                                         op0=ALU.mult, op1=ALU.add).then_inc(denom_ready, 1)

            def h(c):
                d, r, oc = (rec[c.seq][:, n] for n in range(3))
                dve.wait_ge(recip_done, c.count(2, 2))
                dve.tensor_tensor(d, d, r, ALU.mult).then_inc(h_done, 1)
                dve.wait_ge(h_done, c.count(3, 1))
                dve.scalar_tensor_tensor(out=d, in0=d, scalar=2.0, in1=r, op0=ALU.subtract, op1=ALU.mult,
                                         reverse0=True).then_inc(h_done, 1)
                dve.wait_ge(oc_ready, c.count(1, 1))
                dve.wait_ge(h_done, c.count(3, 2))
                dve.tensor_tensor(d, d, oc, ALU.mult).then_inc(h_done, 1)

            def mean_square(c):
                dve.wait_ge(sq_done, c.count(4, 4))
                dve.tensor_scalar(meansq[:, c.seq], sumsq[:, c.seq], 1.0 / D, EPS_RMS, ALU.mult, ALU.add
                                  ).then_inc(ms_ready, 1)

            def residual(c):
                s = c.seq
                dve.wait_ge(rrms_ready, c.count(1, 1))
                for n in range(TT):
                    dve.scalar_tensor_tensor(out=g[:, n], in0=t_ps[:, n // 2, n % 2 * D:n % 2 * D + D],
                                             scalar=rrms[:, s, n:n + 1], in1=scale_bc[:],
                                             op0=ALU.mult, op1=ALU.mult).then_inc(hs_done, 1)
                dve.wait_ge(hs_done, c.count(4, 4))
                dve.wait_ge(res_landed[s], c.of_seq(16))
                dve.tensor_tensor(base[:, s], base[:, s], g[:], ALU.add).then_inc(x1_done, 1)
                dve.wait_ge(x1_done, c.count(1, 1))
                stats(c, base[:, s], bn2, mv2, ln2_stat, 11)
                dve.tensor_scalar(ve2[:, s, 0], mv2[:, :, 1], EPS_LN, None, ALU.add).then_inc(ln2_stat, 1)
                dve.tensor_scalar(ve2[:, s, 1], mv2[:, :, 1], 1.0 + EPS_LN, EPS_LN * EPS_LN, ALU.mult, ALU.add
                                  ).then_inc(ln2_stat, 1)
                dve.tensor_scalar(nm2[:, s], mv2[:, :, 0], -1.0, None, ALU.mult).then_inc(ln2_stat, 1)

            def y_low(c):
                for j in range(KF):
                    if j % 2:
                        dve.wait_ge(silu_done, c.count(8, j + 1))
                        dve.tensor_copy(y_hi[:, j], y[:, j % 3]).then_inc(y_odd_hi, 1)
                        dve.wait_ge(y_odd_hi, c.count(4, j // 2 + 1))
                    else:
                        dve.wait_ge(y_even_hi, c.count(4, j // 2 + 1))
                    dve.tensor_tensor(y_lo[:, j], y[:, j % 3], y_hi[:, j].bitcast(F32), ALU.subtract
                                      ).then_inc(y_lo_done, 1)

            def final(c, u):
                dve.wait_ge(fc2_done, c.count(2, u + 1))
                dve.wait_ge(ln2_norm, c.count(14, 14))
                if c.at >= 1:
                    dve.wait_ge(out_landed[u], c.count(16, 0))
                dve.scalar_tensor_tensor(out=out_sb[:, u], in0=z_ps[:, u], scalar=0.5,
                                         in1=base[:, c.seq, 2 * u:2 * u + 2],
                                         op0=ALU.mult, op1=ALU.add).then_inc(final_done, 1)

            def low_w1():
                dve.wait_ge(w1_rounded, 1)
                dve.tensor_tensor(w1_lo[:], s1[:], w1_hi[:].bitcast(F32), ALU.subtract).then_inc(w1_ready, 1)

            def low_w2():
                dve.wait_ge(w2_rounded, 1)
                dve.tensor_tensor(w2_lo[:], w2_f, w2_hi[:].bitcast(F32), ALU.subtract).then_inc(w2_ready, 1)

            def slot(t):
                ffn, mixed, nxt = t - 2, t - 1, t + 1
                scan_mixed = mixed.exists and not is_slot(mixed, 0) and not early_h(mixed)
                if is_slot(t, 2):
                    dve.wait_ge(beta_w1, 1)
                    dve.tensor_tensor(b1_all[:], z_ps[:, 0, 0, 0:KF], col[:, COL_B1:COL_B1 + KF], ALU.add
                                      ).then_inc(b1_ready, 1)
                if scan_mixed:
                    first_scans(mixed)
                if ffn.exists:
                    low_of(ffn, gt_hi, gt_lo, gt_hi_done, gt_lo_done)
                if scan_mixed:
                    last_scans(mixed)
                if nxt.exists:
                    ln1(nxt)
                if mixed.exists and early_h(t):
                    h(mixed)
                if ffn.exists:
                    y_low(ffn)
                if mixed.exists and not early_h(t):
                    h(mixed)
                if early_h(t):
                    if mixed.exists:
                        mean_square(mixed)
                        residual(mixed)
                if is_slot(t, 0):
                    first_scans(t)
                if ffn.exists:
                    final(ffn, 0)
                if nxt.exists:
                    low_of(nxt, xt_hi, xt_lo, xt_hi_done, xt_lo_done)
                if is_slot(t, 0) or t.exists and early_h(t):
                    if early_h(t):
                        first_scans(t)
                    last_scans(t)
                if mixed.exists and not early_h(t):
                    mean_square(mixed)
                    residual(mixed)
                if ffn.exists:
                    final(ffn, 1)
                if is_slot(t, 1):
                    low_w1()
                    low_w2()

            dve.memset(minus_half[:], -0.5).then_inc(half_ready, 1)
            dve.memset(carry[:, :, 0], 1.0).then_inc(carry_zeroed, 1)
            dve.memset(carry[:, :, 1:3], 0.0).then_inc(carry_zeroed, 1)
            ln1(Chunk(0))
            dve.wait_ge(col_in, 16)
            dve.scalar_tensor_tensor(out=gate_bias[:, 0:2], in0=col[:, 0:2], scalar=1.0,
                                     in1=col[:, COL_IB:COL_IB + KD], op0=ALU.mult, op1=ALU.add).then_inc(bias_ready, 1)
            dve.tensor_scalar(gate_bias[:, 2:4], col[:, 2:4], -1.0, None, ALU.mult)
            dve.tensor_copy(gate_bias[:, 4:6], col[:, 6:8])
            dve.tensor_copy(gate_bias[:, 6:8], col[:, 4:6]).then_inc(bias_ready, 1)
            dve.wait_ge(bias_ready, 2)
            dve.tensor_scalar(gate_bias[:, 0:2], gate_bias[:, 0:2], 1.0 / CAP, None, ALU.mult).then_inc(bias_ready, 1)
            for k in range(KD):
                dve.wait_ge(wg_split_hi, k + 1)
                dve.tensor_tensor(wg_lo[:, k], wg_raw[:, k], wg_hi[:, k].bitcast(F32), ALU.subtract
                                  ).then_inc(wg_split_lo, 1)
            low_of(Chunk(0), xt_hi, xt_lo, xt_hi_done, xt_lo_done)
            dve.wait_ge(row_in, 32)
            run_slots(dve, slot)

        @block.gpsimd
        def _(pool):
            def normalise(dst, src, mul, add, done):
                for n in range(TT):
                    pool.tensor_scalar(dst[:, n], src[:, n], mul[:, n:n + 1], add[:, n:n + 1], ALU.mult, ALU.add
                                       ).then_inc(done, 1)

            def ln1(c):
                s = c.seq
                pool.wait_ge(ln1_stat, c.count(10, 10))
                pool.tensor_tensor(r1[:], ve1[:, s], minus_half[:], ALU.pow).then_inc(ln1_norm, 1)
                pool.wait_ge(ln1_norm, c.count(6, 1))
                pool.tensor_tensor(nr1[:], nm1[:, s], r1[:], ALU.mult).then_inc(ln1_norm, 1)
                wait_apart(pool, ln1_norm, c.count(6, 2), pool_passed)
                if c.at >= 1:
                    wait_apart(pool, xt_ready, (c - 1).count(2, 2), pool_passed)
                normalise(xn, x_in[:, s], r1, nr1, ln1_norm)

            def input_times_z(c):
                r = rec[c.seq]
                pool.wait_ge(i_ready, c.count(1, 1))
                pool.wait_ge(gate_done, c.count(8, 6))
                pool.tensor_tensor(r[:, 2], r[:, 2], r[:, 1], ALU.mult).then_inc(iz_ready, 1)

            def o_times_c(c):
                oc = rec[c.seq][:, 2]
                pool.wait_ge(scan_done, c.count(7, 7))
                pool.wait_ge(gate_done, c.count(8, 8))
                pool.tensor_tensor(oc, oc, o_gate[:, c.seq], ALU.mult).then_inc(oc_ready, 1)

            def rrms_of(c):
                pool.wait_ge(ms_ready, c.count(1, 1))
                pool.tensor_tensor(rrms[:, c.seq], meansq[:, c.seq], minus_half[:], ALU.pow
                                   ).then_inc(rrms_ready, 1)

            def ln2(c):
                s = c.seq
                pool.wait_ge(ln2_stat, c.count(11, 11))
                pool.tensor_tensor(r2[:, 1], ve2[:, s, 1], minus_half[:], ALU.pow).then_inc(ln2_norm, 1)
                pool.wait_ge(ln2_norm, c.count(14, 1))
                pool.tensor_tensor(nr2[:, 1], nm2[:, s], r2[:, 1], ALU.mult).then_inc(ln2_norm, 1)
                wait_apart(pool, ln2_norm, c.count(14, 2), pool_passed)
                normalise(g, base[:, s], r2[:, 1], nr2[:, 1], ln2_norm)
                pool.tensor_tensor(r2[:, 0], ve2[:, s, 0], minus_half[:], ALU.pow).then_inc(ln2_norm, 1)
                pool.wait_ge(ln2_norm, c.count(14, 7))
                pool.tensor_tensor(nr2[:, 0], nm2[:, s], r2[:, 0], ALU.mult).then_inc(ln2_norm, 1)
                pool.tensor_scalar(up2[:], r2[:, 0], 1.0, None, ALU.add).then_inc(ln2_norm, 1)
                wait_apart(pool, ln2_norm, c.count(14, 9), pool_passed)
                normalise(base[:, s], base[:, s], up2, nr2[:, 0], ln2_norm)
                pool.wait_ge(ln2_norm, c.count(14, 13))
                pool.tensor_tensor(base[:, s], base[:, s], b2_bc[:].unsqueeze(1).to_broadcast([P, TT, D]), ALU.add
                                   ).then_inc(ln2_norm, 1)

            def scale_weight(w, by, shifted, landed, done):
                pool.wait_ge(shifted, 1)
                pool.wait_ge(landed, 16)
                pool.tensor_tensor(w, w, by, ALU.mult).then_inc(done, 1)

            def slot(t):
                mixed, nxt = t - 1, t + 1
                if nxt.exists:
                    ln1(nxt)
                if is_slot(t, 0):
                    scale_weight(w1_f, s1[:], w1_shifted, s1_in, w1_scaled)
                    input_times_z(t)
                if mixed.exists:
                    o_times_c(mixed)
                if is_slot(t, 1):
                    scale_weight(w2_f, s2, w2_shifted, s2_in, w2_scaled)
                elif t.exists and t.at > 1:
                    input_times_z(t)
                if mixed.exists:
                    rrms_of(mixed)
                    ln2(mixed)
                if is_slot(t, 1):
                    input_times_z(t)

            pool.memset(ident[:], 0.0).then_inc(ident_ready, 1)
            pool.wait_ge(ident_ready, 1)
            pool.affine_select(out=ident[:], in_=ident[:], compare_op=ALU.not_equal, fill=1.0, base=0,
                               pattern=[[-1, P]], channel_multiplier=1).then_inc(ident_ready, 1)
            pool.wait_ge(half_ready, 1)
            ln1(Chunk(0))
            pool.wait_ge(row_in, 32)
            pool.tensor_scalar(b2_bc[:], b2_bc[:], 0.5, 0.0, ALU.mult, ALU.add).then_inc(half_ready, 1)
            pool.wait_ge(half_ready, 2)
            run_slots(pool, slot)


def kernel(L0_attn_x, L0_attn_W, L0_attn_b, L0_attn_input_bias, L0_attn_scale, L0_ffn_ln_gamma, L0_ffn_ln_beta,
           L0_ffn_fc1_q, L0_ffn_fc1_scales, L0_ffn_fc1_bias, L0_ffn_fc2_q, L0_ffn_fc2_scales, L0_ffn_fc2_bias):
    import numpy as np
    import concourse.bacc as bacc
    from concourse.bass_utils import run_bass_kernel_spmd

    def by_partition(v):
        return np.asarray(v).reshape(-1, P).T

    arrays = {
        "x": np.asarray(L0_attn_x),
        "w_gates": np.asarray(L0_attn_W),
        "cols": np.ascontiguousarray(np.concatenate([by_partition(v) for v in (
            L0_attn_b, L0_attn_input_bias, L0_ffn_ln_gamma, L0_ffn_ln_beta, L0_ffn_fc1_bias)], axis=1)),
        "scale_row": np.asarray(L0_attn_scale),
        "fc1_q": np.asarray(L0_ffn_fc1_q),
        "fc1_scales": np.asarray(L0_ffn_fc1_scales),
        "fc2_q": np.asarray(L0_ffn_fc2_q),
        "fc2_scales": np.asarray(L0_ffn_fc2_scales),
        "b2_row": np.asarray(L0_ffn_fc2_bias),
    }
    nc = bacc.Bacc("TRN2", target_bir_lowering=False, num_devices=1)
    args = [nc.dram_tensor(n, a.shape, mybir.dt.from_np(a.dtype), kind="ExternalInput").ap() for n, a in arrays.items()]
    out = nc.dram_tensor("out", (SEQS, STEPS, D), F32, kind="ExternalOutput").ap()
    layer(nc, *args, out)
    r = run_bass_kernel_spmd(nc, [arrays], core_ids=[0])
    return r.results[0]["out"]
```

```python
from contextlib import ExitStack

import concourse.bass as bass
from concourse import mybir

F32 = mybir.dt.float32
F32R = mybir.dt.float32r
I32 = mybir.dt.int32
ALU = mybir.AluOpType
ACT = mybir.ActivationFunctionType

P = 128
SEQS, STEPS, D = 2, 2048, 256
GATES, F = 4 * D, 1024
T = 512
TT = T // P
CHUNKS = SEQS * STEPS // T
KD = D // P
KF = F // P
GJ = GATES // P
CAP = 10.0
EPS_N, EPS_RMS, EPS_LN = 1e-6, 1e-8, 1e-5
ZERO_POINT = 128.0
GATE_ORDER = [0, 1, 6, 7, 2, 3, 4, 5]
I_TILES, Z_TILES, F_TILES, O_TILES = (0, 1), (2, 3), (4, 5), (6, 7)
COL_B, COL_IB, COL_GAMMA, COL_BETA, COL_B1 = 0, GJ, GJ + KD, GJ + 2 * KD, GJ + 3 * KD
COLS = COL_B1 + KF
LOOP_FROM, LOOP_TO = 3, 7
LAST_SLOT = CHUNKS + 1


class Chunk:

    def __init__(self, at, reg=None):
        self.at, self.reg = at, reg

    def __add__(self, n):
        return Chunk(self.at + n, self.reg)

    def __sub__(self, n):
        return self + -n

    @property
    def exists(self):
        return 0 <= self.at < CHUNKS

    @property
    def seq(self):
        return self.at % SEQS

    def block(self):
        return self.at // SEQS if self.reg is None else self.reg + self.at // SEQS

    def count(self, per, k):
        n = per * self.at + k
        return n if self.reg is None else self.reg * (2 * per) + n

    def of_seq(self, per):
        n = per * (self.at // SEQS + 1)
        return n if self.reg is None else self.reg * per + n


def run_slots(eng, slot):
    for t in range(LOOP_FROM):
        slot(Chunk(t))
    with eng.Fori(0, (LOOP_TO - LOOP_FROM) // 2) as i:
        slot(Chunk(LOOP_FROM, i))
        slot(Chunk(LOOP_FROM + 1, i))
    for t in range(LOOP_TO, LAST_SLOT + 1):
        slot(Chunk(t))


def is_slot(t, n):
    return t.reg is None and t.at == n


def first(c):
    return c.reg is None and c.at == 0


def early_h(t):
    return t.reg is None and t.at >= CHUNKS - 1


def g_by_vector(c):
    return first(c) or early_h(c + 1)


H_AFTER = 6
BIAS_BEFORE = {0: (0, 1, 2, 3), 2: (4, 5), 3: (6, 7)}
EXP_AT = 2


def wait_apart(eng, semaphore, n, passed):
    eng.wait_ge(semaphore, n)
    eng.sem_inc(passed, 1)


def layer(nc, x, w_gates, cols, scale_row, fc1_q, fc1_scales, fc2_q, fc2_scales, b2_row, out):
    x_view = x.rearrange("s (c t p) d -> s c p t d", t=TT, p=P)
    out_view = out.rearrange("s (c t p) d -> s c p t d", t=TT, p=P)

    with ExitStack() as ctx:
        def sb(name, shape, dt=F32):
            return ctx.enter_context(nc.sbuf_tensor(name, shape, dt))

        def ps(name, shape):
            return ctx.enter_context(nc.psum_tensor(name, shape, F32))

        def sem(name):
            return ctx.enter_context(nc.semaphore(name))

        wg_hi = sb("wg_hi", [P, KD, GATES], F32R)
        wg_lo = sb("wg_lo", [P, KD, GATES], F32R)
        w1_hi = sb("w1_hi", [P, KD, F], F32R)
        w1_lo = sb("w1_lo", [P, KD, F], F32R)
        w2_hi = sb("w2_hi", [P, KF, D], F32R)
        w2_lo = sb("w2_lo", [P, KF, D], F32R)
        wg_raw = sb("wg_raw", [P, KD, GATES])
        q1 = sb("q1", [P, KD, F], I32)
        q2 = sb("q2", [P, KF, D], I32)
        s1 = sb("s1", [P, KD, F])
        s2 = wg_raw[:].rearrange("p k (h d) -> p (k h) d", d=D)
        w1_f = q1[:].bitcast(F32)
        w2_f = q2[:].bitcast(F32)
        ident = sb("ident", [P, P])
        col = sb("col", [P, COLS])
        gate_bias = sb("gate_bias", [P, GJ])
        b1_all = sb("b1_all", [P, KF])
        scale_bc = sb("scale_bc", [P, D])
        b2_bc = sb("b2_bc", [P, D])
        x_in = sb("x_in", [P, 2, TT, D])
        xn = sb("xn", [P, TT, D])
        g = sb("g", [P, TT, D])
        base = sb("base", [P, 2, TT, D])
        out_sb = sb("out_sb", [P, 2, 2, D])
        xt_hi = sb("xt_hi", [P, KD, T], F32R)
        xt_lo = sb("xt_lo", [P, KD, T], F32R)
        gt_hi = sb("gt_hi", [P, KD, T], F32R)
        gt_lo = sb("gt_lo", [P, KD, T], F32R)
        y = sb("y", [P, 3, T])
        y_hi = sb("y_hi", [P, KF, T], F32R)
        y_lo = sb("y_lo", [P, KF, T], F32R)
        rec = [sb(f"rec{s}", [P, 3, KD, T]) for s in range(2)]
        f_gate = sb("f_gate", [P, 2, KD, T])
        o_gate = sb("o_gate", [P, 2, KD, T])
        carry = sb("carry", [P, 2, 3, KD])
        bn1 = sb("bn1", [P, TT, 6])
        mv1 = sb("mv1", [P, TT, 2])
        ve1 = sb("ve1", [P, 2, TT])
        nm1 = sb("nm1", [P, 2, TT])
        r1 = sb("r1", [P, TT])
        nr1 = sb("nr1", [P, TT])
        bn2 = sb("bn2", [P, TT, 6])
        mv2 = sb("mv2", [P, TT, 2])
        ve2 = sb("ve2", [P, 2, 2, TT])
        nm2 = sb("nm2", [P, 2, TT])
        r2 = sb("r2", [P, 2, TT])
        nr2 = sb("nr2", [P, 2, TT])
        up2 = sb("up2", [P, TT])
        sumsq = sb("sumsq", [P, 2, TT])
        meansq = sb("meansq", [P, 2, TT])
        rrms = sb("rrms", [P, 2, TT])
        minus_half = sb("minus_half", [P, TT])

        mm_ps = ps("mm_ps", [P, 4, T])
        z_ps = ps("z_ps", [P, 2, 2, D])
        t_ps = ps("t_ps", [P, 2, T])

        def h_bank(c, u):
            return z_ps[:, u].rearrange("p n d -> p (n d)") if first(c) else t_ps[:, u]

        ident_ready = sem("ident_ready")
        half_ready = sem("half_ready")
        wg_in = [sem(f"wg_in{k}") for k in range(KD)]
        q1_in, q2_in, s1_in, col_in, row_in = (sem(n) for n in (
            "q1_in", "q2_in", "s1_in", "col_in", "row_in"))
        s2_in = sem("s2_in")
        bias_ready = sem("bias_ready")
        carry_zeroed = sem("carry_zeroed")
        wg_split_hi, wg_split_lo = sem("wg_split_hi"), sem("wg_split_lo")
        w1_scaled, w1_gamma, w1_rounded, w1_ready = (sem(n) for n in (
            "w1_scaled", "w1_gamma", "w1_rounded", "w1_ready"))
        w2_scaled, w2_rounded, w2_ready = (sem(n) for n in ("w2_scaled", "w2_rounded", "w2_ready"))
        beta_w1 = sem("beta_w1")
        b1_ready = sem("b1_ready")
        x_half_landed = sem("x_half_landed")
        x_landed = [sem(f"x_landed{s}") for s in range(2)]
        res_landed = [sem(f"res_landed{s}") for s in range(2)]
        out_landed = [sem(f"out_landed{u}") for u in range(2)]
        ln1_stat = sem("ln1_stat")
        ln1_norm = sem("ln1_norm")
        xt_ready = sem("xt_ready")
        xt_hi_done = sem("xt_hi_done")
        xt_lo_done = sem("xt_lo_done")
        pre_done = sem("pre_done")
        gate_done = sem("gate_done")
        i_ready = sem("i_ready")
        iz_ready = sem("iz_ready")
        scan_done = sem("scan_done")
        denom_ready = sem("denom_ready")
        recip_done = sem("recip_done")
        oc_ready = sem("oc_ready")
        h_done = sem("h_done")
        ht_ready = sem("ht_ready")
        sq_done = sem("sq_done")
        ms_ready = sem("ms_ready")
        rrms_ready = sem("rrms_ready")
        hs_done = sem("hs_done")
        x1_done = sem("x1_done")
        ln2_stat = sem("ln2_stat")
        ln2_norm = sem("ln2_norm")
        gt_ready = sem("gt_ready")
        gt_hi_done = sem("gt_hi_done")
        gt_lo_done = sem("gt_lo_done")
        fc1_done = sem("fc1_done")
        silu_done = sem("silu_done")
        y_even_hi = sem("y_even_hi")
        y_odd_hi = sem("y_odd_hi")
        y_lo_done = sem("y_lo_done")
        fc2_done = sem("fc2_done")
        final_done = sem("final_done")

        sp_passed, dve_passed, pool_passed = sem("sp_passed"), sem("dve_passed"), sem("pool_passed")

        block = ctx.enter_context(nc.Block())

        @block.sync
        def _(sp):
            def load_x(c):
                if c.at >= 2:
                    wait_apart(sp, ln1_norm, (c - 2).count(6, 6), sp_passed)
                sp.dma_start(x_in[:, c.seq], x_view[c.seq, bass.ds(c.block(), 1)].rearrange("c p t d -> (c p) t d")
                             ).then_inc(x_landed[c.seq], 16)

            sp.dma_start(x_in[:, 0, 0:2], x_view[0, 0, :, 0:2]).then_inc(x_half_landed, 16)
            sp.dma_start(x_in[:, 0, 2:TT], x_view[0, 0, :, 2:TT]).then_inc(x_landed[0], 16)
            for k in range(KD):
                sp.dma_start(wg_raw[:, k], w_gates[k * P:(k + 1) * P, :]).then_inc(wg_in[k], 16)
            sp.dma_start(x_in[:, 1], x_view[1, 0]).then_inc(x_landed[1], 16)
            sp.dma_start(q1[:], fc1_q.rearrange("(k p) f -> p k f", p=P)).then_inc(q1_in, 16)
            sp.dma_start(s1[:], fc1_scales.partition_broadcast(P)).then_inc(s1_in, 16)
            sp.dma_start(q2[:], fc2_q.rearrange("(k p) f -> p k f", p=P)).then_inc(q2_in, 16)
            sp.wait_ge(wg_split_lo, KD)
            sp.dma_start(s2, fc2_scales.partition_broadcast(P)).then_inc(s2_in, 16)

            def slot(t):
                if (t + 1).exists and not (t.reg is None and t.at == 0):
                    load_x(t + 1)
                c = t - 2
                if c.exists:
                    for u in range(2):
                        wait_apart(sp, final_done, c.count(2, u + 1), sp_passed)
                        sp.dma_start(
                            out_view[c.seq, bass.ds(c.block(), 1), :, 2 * u:2 * u + 2].rearrange("c p t d -> (c p) t d"),
                            out_sb[:, u]).then_inc(out_landed[u], 16)
                if t.exists:
                    sp.dma_start(base[:, t.seq], x_view[t.seq, bass.ds(t.block(), 1)].rearrange("c p t d -> (c p) t d")
                                 ).then_inc(res_landed[t.seq], 16)

            run_slots(sp, slot)
            for u in range(2):
                sp.wait_ge(out_landed[u], 16 * CHUNKS)

        @block.tensor
        def _(pe):
            def three_passes(dst, w_pair, w_at, a_pair, a_at, first, last):
                (wh, wl), (ah, al) = w_pair, a_pair
                pe.matmul(dst, wh[w_at], ah[a_at], start=first, stop=False)
                pe.matmul(dst, wh[w_at], al[a_at], start=False, stop=False)
                return pe.matmul(dst, wl[w_at], ah[a_at], start=False, stop=last)

            def first_tile(c, dst, w_pair, w_at, a_pair, hi_done, lo_done):
                (wh, wl), (ah, al) = w_pair, a_pair
                for k in range(KD):
                    pe.wait_ge(hi_done, c.count(2, k + 1))
                    if first(c) and wh is wg_hi:
                        pe.wait_ge(wg_split_lo, k + 1)
                    pe.matmul(dst, wh[:, k, w_at], ah[:, k], start=(k == 0), stop=False)
                    pe.matmul(dst, wl[:, k, w_at], ah[:, k], start=False, stop=False)
                for k in range(KD):
                    pe.wait_ge(lo_done, c.count(2, k + 1))
                    ins = pe.matmul(dst, wh[:, k, w_at], al[:, k], start=False, stop=(k == KD - 1))
                return ins

            def turn_back(src, ready):
                for k in range(KD):
                    yield k
                    for n in range(TT):
                        ins = pe.transpose(t_ps[:, k, n * P:(n + 1) * P], src[:, n, k * P:(k + 1) * P], ident[:])
                    ins.then_inc(ready, 1)

            def x_turned(c):
                pe.wait_ge(ln1_norm, c.count(6, 6))
                for k in turn_back(xn, xt_ready):
                    if c.at >= 3:
                        pe.wait_ge(gt_lo_done, (c - 3).count(2, k + 1))
                    elif c.at >= 1:
                        pe.wait_ge(xt_lo_done, (c - 1).count(2, k + 1))

            def g_turned(c):
                pe.wait_ge(ln2_norm, c.count(14, 6))
                for k in turn_back(g, gt_ready):
                    if first(c):
                        pe.wait_ge(xt_lo_done, (c + 2).count(2, k + 1))
                    else:
                        pe.wait_ge(hs_done, c.count(4, 2 * k + 2))

            def h_turned(c):
                pe.wait_ge(h_done, c.count(3, 3))
                for u in range(2):
                    if first(c):
                        pe.wait_ge(b1_ready, 1)
                    elif (c + 2).exists:
                        pe.wait_ge(xt_lo_done, (c + 2).count(2, u + 1))
                    else:
                        pe.wait_ge(gt_lo_done, (c - 1).count(2, u + 1))
                    for n in range(2):
                        for k in range(KD):
                            at = (2 * n + k) * P
                            tok = (2 * u + n) * P
                            ins = pe.transpose(h_bank(c, u)[:, at:at + P], rec[c.seq][:, 0, k, tok:tok + P], ident[:])
                    ins.then_inc(ht_ready, 1)

            def gate_products(c, tiles):
                for j in tiles:
                    if j >= 4:
                        pe.wait_ge(gate_done, c.count(8, j - 3))
                    elif c.at >= 3:
                        pe.wait_ge(silu_done, (c - 3).count(8, j + 5))
                    elif c.at >= 1:
                        pe.wait_ge(gate_done, (c - 1).count(8, j + 5))
                    f = GATE_ORDER[j] * P
                    if j == 0:
                        first_tile(c, mm_ps[:, 0], (wg_hi, wg_lo), slice(f, f + P), (xt_hi, xt_lo),
                                   xt_hi_done, xt_lo_done).then_inc(pre_done, 1)
                        continue
                    for k in range(KD):
                        ins = three_passes(mm_ps[:, j % 4], (wg_hi, wg_lo), (slice(None), k, slice(f, f + P)),
                                           (xt_hi, xt_lo), (slice(None), k), k == 0, k == KD - 1)
                    ins.then_inc(pre_done, 1)

            def shifted_bias(tiles):
                pe.wait_ge(w1_scaled, 1)
                for j in tiles:
                    for k in range(KD):
                        ins = pe.matmul(z_ps[:, 0, 0, j:j + 1], w1_f[:, k, j * P:(j + 1) * P],
                                        col[:, COL_BETA + k:COL_BETA + k + 1], start=(k == 0), stop=(k == KD - 1))
                ins.then_inc(beta_w1, 1)

            def fc1(c, tiles):
                if c.reg is None and c.at == 0:
                    pe.wait_ge(w1_ready, 1)
                    pe.wait_ge(w2_ready, 1)
                for j in tiles:
                    if j >= 4:
                        pe.wait_ge(silu_done, c.count(8, j - 3))
                    elif (c + 2).exists:
                        pe.wait_ge(gate_done, (c + 2).count(8, j + 5))
                    else:
                        pe.wait_ge(silu_done, (c - 1).count(8, j + 5))
                    if j == 0:
                        first_tile(c, mm_ps[:, 0], (w1_hi, w1_lo), slice(0, P), (gt_hi, gt_lo),
                                   gt_hi_done, gt_lo_done).then_inc(fc1_done, 1)
                        continue
                    for k in range(KD):
                        ins = three_passes(mm_ps[:, j % 4], (w1_hi, w1_lo), (slice(None), k, slice(j * P, j * P + P)),
                                           (gt_hi, gt_lo), (slice(None), k), k == 0, k == KD - 1)
                    ins.then_inc(fc1_done, 1)

            def fc2(c, n):
                u = n // 2
                if n % 2 == 0:
                    if c.at >= 1:
                        pe.wait_ge(final_done, (c - 1).count(2, u + 1))
                    else:
                        pe.wait_ge(hs_done, 2 * u + 2)
                for k in range(KF):
                    if n == 0:
                        pe.wait_ge(y_lo_done, c.count(8, k + 1))
                    ins = three_passes(z_ps[:, u, n % 2], (y_hi, y_lo), (slice(None), k, slice(n * P, n * P + P)),
                                       (w2_hi, w2_lo), (slice(None), k), k == 0, k == KF - 1)
                if n % 2:
                    ins.then_inc(fc2_done, 1)

            def slot(t):
                ffn, mixed, nxt = t - 2, t - 1, t + 1
                if is_slot(t, 1):
                    for j in range(7):
                        if j in BIAS_BEFORE:
                            shifted_bias(BIAS_BEFORE[j])
                        gate_products(t, (j,))
                    h_turned(mixed)
                elif t.exists:
                    gate_products(t, range(0, 7))
                if not ffn.exists:
                    x_turned(nxt)
                    gate_products(t, range(7, GJ))
                    return
                g_turned(ffn)
                if t.exists:
                    gate_products(t, range(7, GJ))
                if mixed.exists and early_h(t):
                    fc1(ffn, range(H_AFTER))
                    h_turned(mixed)
                    fc1(ffn, range(H_AFTER, KF))
                else:
                    fc1(ffn, range(KF))
                fc2(ffn, 0)
                fc2(ffn, 1)
                if nxt.exists:
                    x_turned(nxt)
                fc2(ffn, 2)
                if mixed.exists and not early_h(t):
                    h_turned(mixed)
                fc2(ffn, 3)

            pe.wait_ge(ident_ready, 2)
            for n in range(TT):
                pe.wait_ge(ln1_norm, 2 + n + 1)
                for k in range(KD):
                    ins = pe.transpose(t_ps[:, k, n * P:(n + 1) * P], xn[:, n, k * P:(k + 1) * P], ident[:])
                    if n == TT - 1:
                        ins.then_inc(xt_ready, 1)
            run_slots(pe, slot)

        @block.scalar
        def _(act):
            act.dma_start(col[:], cols).then_inc(col_in, 16)
            act.dma_start(scale_bc[:], scale_row.partition_broadcast(P)).then_inc(row_in, 16)
            act.dma_start(b2_bc[:], b2_row.partition_broadcast(P)).then_inc(row_in, 16)
            act.preload_act_table_set("sigmoid_and_others")

            def high_of(c, hi, ready, done):
                for k in range(KD):
                    act.wait_ge(ready, c.count(2, k + 1))
                    act.activation(hi[:, k], t_ps[:, k], ACT.Copy).then_inc(done, 1)

            def gates(c, tiles):
                s = c.seq
                for j in tiles:
                    if c.at >= 2 and j in (I_TILES[0], Z_TILES[0]):
                        act.wait_ge(h_done, (c - 2).count(3, 2 if j == I_TILES[0] else 3))
                    act.wait_ge(pre_done, c.count(8, j + 1))
                    bias, tile = gate_bias[:, j:j + 1], mm_ps[:, j % 4]
                    if j in I_TILES:
                        ins = act.activation(rec[s][:, 1, j], tile, ACT.Tanh, bias=bias, scale=1.0 / CAP)
                    elif j in F_TILES:
                        ins = act.activation(f_gate[:, s, j - 4], tile, ACT.Sigmoid, bias=bias, scale=-1.0)
                    elif j in Z_TILES:
                        ins = act.activation(rec[s][:, 2, j - 2], tile, ACT.Tanh, bias=bias)
                    else:
                        ins = act.activation(o_gate[:, s, j - 6], tile, ACT.Sigmoid, bias=bias)
                    ins.then_inc(gate_done, 1)

            def exp_i(c):
                act.wait_ge(gate_done, c.count(8, 2))
                act.activation(rec[c.seq][:, 1], rec[c.seq][:, 1], ACT.Exp, scale=CAP).then_inc(i_ready, 1)

            def reciprocal(c):
                r = rec[c.seq][:, 1]
                act.wait_ge(denom_ready, c.count(1, 1))
                act.activation(r, rec[c.seq][:, 0], ACT.Ln).then_inc(recip_done, 1)
                act.wait_ge(recip_done, c.count(2, 1))
                act.activation(r, r, ACT.Exp, scale=-1.0).then_inc(recip_done, 1)

            def square_sums(c):
                if c.at >= 1:
                    act.wait_ge(gt_ready, (c - 1).count(2, 2))
                for n in range(TT):
                    if n % 2 == 0:
                        act.wait_ge(ht_ready, c.count(2, n // 2 + 1))
                    act.activation(g[:, n], h_bank(c, n // 2)[:, n % 2 * D:n % 2 * D + D], ACT.Square,
                                   accum_out=sumsq[:, c.seq, n:n + 1]).then_inc(sq_done, 1)

            def silu(c):
                for j in range(KF):
                    act.wait_ge(fc1_done, c.count(8, j + 1))
                    if c.at >= 1 or j >= 3:
                        act.wait_ge(y_lo_done, c.count(8, j - 2))
                    act.activation(y[:, j % 3], mm_ps[:, j % 4], ACT.Silu, bias=b1_all[:, j:j + 1]
                                   ).then_inc(silu_done, 1)
                    if j % 2 == 0:
                        act.wait_ge(silu_done, c.count(8, j + 1))
                        act.activation(y_hi[:, j], y[:, j % 3], ACT.Copy).then_inc(y_even_hi, 1)

            def slot(t):
                ffn, mixed, nxt = t - 2, t - 1, t + 1
                if is_slot(t, 0):
                    gates(t, I_TILES)
                    act.preload_act_table_set("natural_log_exp_and_others")
                    exp_i(t)
                    act.preload_act_table_set("sigmoid_and_others")
                    gates(t, range(2, 7))
                elif is_slot(t, 1) or t.exists and early_h(t):
                    if not is_slot(t, 1):
                        act.preload_act_table_set("sigmoid_and_others")
                    exp_at = 2 if is_slot(t, 1) else EXP_AT
                    gates(t, range(exp_at))
                    act.preload_act_table_set("natural_log_exp_and_others")
                    if is_slot(t, 1):
                        reciprocal(mixed)
                    exp_i(t)
                    act.preload_act_table_set("sigmoid_and_others")
                    gates(t, range(exp_at, 7))
                if not ffn.exists:
                    if is_slot(t, 1):
                        square_sums(mixed)
                    act.wait_ge(pre_done, t.count(8, 8))
                    high_of(nxt, xt_hi, xt_ready, xt_hi_done)
                    gates(t, range(7, GJ))
                    return
                if t.exists and not early_h(t):
                    if not is_slot(t, 2):
                        act.preload_act_table_set("sigmoid_and_others")
                    gates(t, range(0, 7))
                high_of(ffn, gt_hi, gt_ready, gt_hi_done)
                if t.exists:
                    gates(t, range(7, GJ))
                if mixed.exists and early_h(t):
                    act.preload_act_table_set("natural_log_exp_and_others")
                    reciprocal(mixed)
                if is_slot(t, 2):
                    act.wait_ge(b1_ready, 1)
                act.preload_act_table_set("silu_and_others")
                silu(ffn)
                if mixed.exists and early_h(t):
                    square_sums(mixed)
                if early_h(t):
                    return
                act.preload_act_table_set("natural_log_exp_and_others")
                reciprocal(mixed)
                exp_i(t)
                if nxt.exists:
                    high_of(nxt, xt_hi, xt_ready, xt_hi_done)
                square_sums(mixed)

            for k in range(KD):
                act.wait_ge(wg_in[k], 16)
                act.activation(wg_hi[:, k], wg_raw[:, k], ACT.Copy).then_inc(wg_split_hi, 1)
            high_of(Chunk(0), xt_hi, xt_ready, xt_hi_done)
            act.wait_ge(bias_ready, 3)
            run_slots(act, slot)

        @block.vector
        def _(dve):
            def stats(c, src, bn, mv, done, per):
                for n in range(TT):
                    if first(c) and bn is bn1 and n == 2:
                        dve.wait_ge(x_landed[0], 16)
                    dve.bn_stats(bn[:, n], src[:, n]).then_inc(done, 1)
                wait_apart(dve, done, c.count(per, TT), dve_passed)
                for n in range(TT):
                    dve.bn_aggr(mv[:, n], bn[:, n]).then_inc(done, 1)
                dve.wait_ge(done, c.count(per, 2 * TT))

            def ln1(c):
                s = c.seq
                if first(c):
                    dve.wait_ge(x_half_landed, 16)
                else:
                    dve.wait_ge(x_landed[s], c.of_seq(16))
                stats(c, x_in[:, s], bn1, mv1, ln1_stat, 10)
                if c.at >= 2:
                    dve.wait_ge(ln1_norm, (c - 2).count(6, 2))
                dve.tensor_scalar(ve1[:, s], mv1[:, :, 1], EPS_LN, None, ALU.add).then_inc(ln1_stat, 1)
                dve.tensor_scalar(nm1[:, s], mv1[:, :, 0], -1.0, None, ALU.mult).then_inc(ln1_stat, 1)

            def low_of(c, hi, lo, hi_done, done):
                for k in range(KD):
                    dve.wait_ge(hi_done, c.count(2, k + 1))
                    dve.tensor_tensor(lo[:, k], t_ps[:, k], hi[:, k].bitcast(F32), ALU.subtract).then_inc(done, 1)

            def maximum_scans(c):
                s = c.seq
                r, fg = rec[s], f_gate[:, s]
                dve.wait_ge(i_ready, c.count(1, 1))
                if c.at >= 2:
                    dve.wait_ge(ht_ready, (c - 2).count(2, 2))
                    dve.wait_ge(scan_done, (c - 2).count(7, 7))
                else:
                    dve.wait_ge(carry_zeroed, 2)
                dve.wait_ge(gate_done, c.count(8, 6))
                for k in range(KD):
                    dve.tensor_tensor_scan(r[:, 0, k], fg[:, k], r[:, 1, k], carry[:, s, 0, k:k + 1],
                                           ALU.mult, ALU.max).then_inc(scan_done, 1)

            def denominator_scans(c, blocks):
                s = c.seq
                r, fg = rec[s], f_gate[:, s]
                dve.wait_ge(iz_ready, c.count(1, 1))
                for k in blocks:
                    dve.tensor_tensor_scan(r[:, 1, k], fg[:, k], r[:, 1, k], carry[:, s, 1, k:k + 1],
                                           ALU.mult, ALU.add).then_inc(scan_done, 1)

            def first_scans(c):
                maximum_scans(c)
                denominator_scans(c, range(KD))

            def last_scans(c):
                numerator_scans(c)
                denominator(c)

            def numerator_scans(c):
                s = c.seq
                r, fg = rec[s], f_gate[:, s]
                for k in range(KD):
                    dve.tensor_tensor_scan(r[:, 2, k], fg[:, k], r[:, 2, k], carry[:, s, 2, k:k + 1],
                                           ALU.mult, ALU.add).then_inc(scan_done, 1)

            def denominator(c):
                s = c.seq
                r = rec[s]
                dve.wait_ge(scan_done, c.count(7, 6))
                dve.tensor_copy(carry[:, s], r[:, :, :, T - 1]).then_inc(scan_done, 1)
                dve.wait_ge(scan_done, c.count(7, 7))
                dve.scalar_tensor_tensor(out=r[:, 0], in0=r[:, 0], scalar=EPS_N, in1=r[:, 1],
                                         op0=ALU.mult, op1=ALU.add).then_inc(denom_ready, 1)

            def h(c):
                d, r, oc = (rec[c.seq][:, n] for n in range(3))
                dve.wait_ge(recip_done, c.count(2, 2))
                dve.tensor_tensor(d, d, r, ALU.mult).then_inc(h_done, 1)
                dve.wait_ge(h_done, c.count(3, 1))
                dve.scalar_tensor_tensor(out=d, in0=d, scalar=2.0, in1=r, op0=ALU.subtract, op1=ALU.mult,
                                         reverse0=True).then_inc(h_done, 1)
                dve.wait_ge(oc_ready, c.count(1, 1))
                dve.wait_ge(h_done, c.count(3, 2))
                dve.tensor_tensor(d, d, oc, ALU.mult).then_inc(h_done, 1)

            def mean_square(c):
                dve.wait_ge(sq_done, c.count(4, 4))
                dve.tensor_scalar(meansq[:, c.seq], sumsq[:, c.seq], 1.0 / D, EPS_RMS, ALU.mult, ALU.add
                                  ).then_inc(ms_ready, 1)

            def residual(c):
                s = c.seq
                dve.wait_ge(rrms_ready, c.count(1, 1))
                for n in range(TT):
                    dve.scalar_tensor_tensor(out=g[:, n], in0=h_bank(c, n // 2)[:, n % 2 * D:n % 2 * D + D],
                                             scalar=rrms[:, s, n:n + 1], in1=scale_bc[:],
                                             op0=ALU.mult, op1=ALU.mult).then_inc(hs_done, 1)
                dve.wait_ge(hs_done, c.count(4, 4))
                dve.wait_ge(res_landed[s], c.of_seq(16))
                dve.tensor_tensor(base[:, s], base[:, s], g[:], ALU.add).then_inc(x1_done, 1)
                dve.wait_ge(x1_done, c.count(1, 1))
                stats(c, base[:, s], bn2, mv2, ln2_stat, 11)
                dve.tensor_scalar(ve2[:, s, 0], mv2[:, :, 1], EPS_LN, None, ALU.add).then_inc(ln2_stat, 1)
                dve.tensor_scalar(ve2[:, s, 1], mv2[:, :, 1], 1.0 + EPS_LN, EPS_LN * EPS_LN, ALU.mult, ALU.add
                                  ).then_inc(ln2_stat, 1)
                dve.tensor_scalar(nm2[:, s], mv2[:, :, 0], -1.0, None, ALU.mult).then_inc(ln2_stat, 1)

            def g_normalised(c):
                dve.wait_ge(ln2_norm, c.count(14, 2))
                for n in range(TT):
                    dve.tensor_scalar(g[:, n], base[:, c.seq, n], r2[:, 1, n:n + 1], nr2[:, 1, n:n + 1],
                                      ALU.mult, ALU.add).then_inc(ln2_norm, 1)

            def y_low(c):
                for j in range(KF):
                    if j % 2:
                        dve.wait_ge(silu_done, c.count(8, j + 1))
                        dve.tensor_copy(y_hi[:, j], y[:, j % 3]).then_inc(y_odd_hi, 1)
                        dve.wait_ge(y_odd_hi, c.count(4, j // 2 + 1))
                    else:
                        dve.wait_ge(y_even_hi, c.count(4, j // 2 + 1))
                    dve.tensor_tensor(y_lo[:, j], y[:, j % 3], y_hi[:, j].bitcast(F32), ALU.subtract
                                      ).then_inc(y_lo_done, 1)

            def final(c, u):
                dve.wait_ge(fc2_done, c.count(2, u + 1))
                dve.wait_ge(ln2_norm, c.count(14, 14))
                if c.at >= 1:
                    dve.wait_ge(out_landed[u], c.count(16, 0))
                dve.scalar_tensor_tensor(out=out_sb[:, u], in0=z_ps[:, u], scalar=0.5,
                                         in1=base[:, c.seq, 2 * u:2 * u + 2],
                                         op0=ALU.mult, op1=ALU.add).then_inc(final_done, 1)

            def split_w1():
                dve.wait_ge(q1_in, 16)
                dve.wait_ge(s1_in, 16)
                dve.scalar_tensor_tensor(out=w1_f, in0=q1[:], scalar=-ZERO_POINT, in1=s1[:],
                                         op0=ALU.add, op1=ALU.mult).then_inc(w1_scaled, 1)
                dve.wait_ge(w1_scaled, 1)
                for k in range(KD):
                    dve.tensor_scalar(s1[:, k], w1_f[:, k], col[:, COL_GAMMA + k:COL_GAMMA + k + 1], None, ALU.mult
                                      ).then_inc(w1_gamma, 1)
                dve.wait_ge(w1_gamma, KD)
                dve.tensor_copy(w1_hi[:], s1[:]).then_inc(w1_rounded, 1)
                dve.wait_ge(w1_rounded, 1)
                dve.tensor_tensor(w1_lo[:], s1[:], w1_hi[:].bitcast(F32), ALU.subtract).then_inc(w1_ready, 1)

            def high_w2():
                dve.wait_ge(q2_in, 16)
                dve.wait_ge(s2_in, 16)
                dve.scalar_tensor_tensor(out=w2_f, in0=q2[:], scalar=-ZERO_POINT, in1=s2,
                                         op0=ALU.add, op1=ALU.mult).then_inc(w2_scaled, 1)
                dve.wait_ge(w2_scaled, 1)
                dve.tensor_copy(w2_hi[:], w2_f).then_inc(w2_rounded, 1)

            def slot(t):
                ffn, mixed, nxt = t - 2, t - 1, t + 1
                if is_slot(t, 0):
                    ln1(nxt)
                    split_w1()
                    maximum_scans(t)
                    denominator_scans(t, range(1))
                    low_of(nxt, xt_hi, xt_lo, xt_hi_done, xt_lo_done)
                    denominator_scans(t, range(1, KD))
                    last_scans(t)
                    return
                if is_slot(t, 1):
                    ln1(nxt)
                    dve.wait_ge(beta_w1, len(BIAS_BEFORE))
                    dve.tensor_tensor(b1_all[:], z_ps[:, 0, 0, 0:KF], col[:, COL_B1:COL_B1 + KF], ALU.add
                                      ).then_inc(b1_ready, 1)
                    h(mixed)
                    high_w2()
                    mean_square(mixed)
                    low_of(nxt, xt_hi, xt_lo, xt_hi_done, xt_lo_done)
                    residual(mixed)
                    maximum_scans(t)
                    g_normalised(mixed)
                    return
                if is_slot(t, 2):
                    denominator_scans(mixed, range(KD))
                elif not early_h(mixed):
                    denominator_scans(mixed, range(1, KD))
                if early_h(t):
                    if t.exists:
                        last_scans(mixed)
                    low_of(ffn, gt_hi, gt_lo, gt_hi_done, gt_lo_done)
                    if not t.exists:
                        final(ffn - 1, 0)
                        final(ffn - 1, 1)
                    if t.exists:
                        first_scans(t)
                    if mixed.exists:
                        h(mixed)
                    y_low(ffn)
                    if mixed.exists:
                        mean_square(mixed)
                    if t.exists:
                        numerator_scans(t)
                    if mixed.exists:
                        residual(mixed)
                    if t.exists:
                        denominator(t)
                    if mixed.exists:
                        g_normalised(mixed)
                    if not mixed.exists:
                        final(ffn, 0)
                        final(ffn, 1)
                    return
                low_of(ffn, gt_hi, gt_lo, gt_hi_done, gt_lo_done)
                last_scans(mixed)
                if nxt.exists:
                    ln1(nxt)
                y_low(ffn)
                h(mixed)
                if nxt.exists:
                    low_of(nxt, xt_hi, xt_lo, xt_hi_done, xt_lo_done)
                maximum_scans(t)
                mean_square(mixed)
                denominator_scans(t, range(1))
                residual(mixed)
                final(ffn, 0)
                final(ffn, 1)

            dve.memset(minus_half[:], -0.5).then_inc(half_ready, 1)
            dve.memset(carry[:, :, 0], 1.0).then_inc(carry_zeroed, 1)
            dve.memset(carry[:, :, 1:3], 0.0).then_inc(carry_zeroed, 1)
            ln1(Chunk(0))
            dve.wait_ge(col_in, 16)
            dve.scalar_tensor_tensor(out=gate_bias[:, 0:2], in0=col[:, 0:2], scalar=1.0,
                                     in1=col[:, COL_IB:COL_IB + KD], op0=ALU.mult, op1=ALU.add).then_inc(bias_ready, 1)
            dve.tensor_scalar(gate_bias[:, 4:6], col[:, 2:4], -1.0, None, ALU.mult)
            dve.tensor_copy(gate_bias[:, 2:4], col[:, 6:8])
            dve.tensor_copy(gate_bias[:, 6:8], col[:, 4:6]).then_inc(bias_ready, 1)
            dve.wait_ge(bias_ready, 2)
            dve.tensor_scalar(gate_bias[:, 0:2], gate_bias[:, 0:2], 1.0 / CAP, None, ALU.mult).then_inc(bias_ready, 1)
            dve.wait_ge(ln1_norm, 2)
            for n in range(TT):
                dve.tensor_scalar(xn[:, n], x_in[:, 0, n], r1[:, n:n + 1], nr1[:, n:n + 1], ALU.mult, ALU.add
                                  ).then_inc(ln1_norm, 1)
            for k in range(KD):
                dve.wait_ge(wg_split_hi, k + 1)
                dve.tensor_tensor(wg_lo[:, k], wg_raw[:, k], wg_hi[:, k].bitcast(F32), ALU.subtract
                                  ).then_inc(wg_split_lo, 1)
            low_of(Chunk(0), xt_hi, xt_lo, xt_hi_done, xt_lo_done)
            dve.wait_ge(row_in, 32)
            run_slots(dve, slot)

        @block.gpsimd
        def _(pool):
            def normalise(dst, src, mul, add, done):
                for n in range(TT):
                    pool.tensor_scalar(dst[:, n], src[:, n], mul[:, n:n + 1], add[:, n:n + 1], ALU.mult, ALU.add
                                       ).then_inc(done, 1)

            def ln1(c):
                s = c.seq
                pool.wait_ge(ln1_stat, c.count(10, 10))
                pool.tensor_tensor(r1[:], ve1[:, s], minus_half[:], ALU.pow).then_inc(ln1_norm, 1)
                pool.wait_ge(ln1_norm, c.count(6, 1))
                pool.tensor_tensor(nr1[:], nm1[:, s], r1[:], ALU.mult).then_inc(ln1_norm, 1)
                if first(c):
                    return
                wait_apart(pool, ln1_norm, c.count(6, 2), pool_passed)
                if c.at >= 1:
                    wait_apart(pool, xt_ready, (c - 1).count(2, 2), pool_passed)
                normalise(xn, x_in[:, s], r1, nr1, ln1_norm)

            def input_times_z(c):
                r = rec[c.seq]
                pool.wait_ge(i_ready, c.count(1, 1))
                pool.wait_ge(gate_done, c.count(8, 4))
                pool.tensor_tensor(r[:, 2], r[:, 2], r[:, 1], ALU.mult).then_inc(iz_ready, 1)

            def o_times_c(c):
                oc = rec[c.seq][:, 2]
                pool.wait_ge(scan_done, c.count(7, 7))
                pool.wait_ge(gate_done, c.count(8, 8))
                pool.tensor_tensor(oc, oc, o_gate[:, c.seq], ALU.mult).then_inc(oc_ready, 1)

            def rrms_of(c):
                pool.wait_ge(ms_ready, c.count(1, 1))
                pool.tensor_tensor(rrms[:, c.seq], meansq[:, c.seq], minus_half[:], ALU.pow
                                   ).then_inc(rrms_ready, 1)

            def ln2_g(c):
                s = c.seq
                pool.wait_ge(ln2_stat, c.count(11, 11))
                pool.tensor_tensor(r2[:, 1], ve2[:, s, 1], minus_half[:], ALU.pow).then_inc(ln2_norm, 1)
                pool.wait_ge(ln2_norm, c.count(14, 1))
                pool.tensor_tensor(nr2[:, 1], nm2[:, s], r2[:, 1], ALU.mult).then_inc(ln2_norm, 1)
                wait_apart(pool, ln2_norm, c.count(14, 2), pool_passed)
                if not g_by_vector(c):
                    normalise(g, base[:, s], r2[:, 1], nr2[:, 1], ln2_norm)

            def ln2_base(c):
                s = c.seq
                pool.wait_ge(ln2_norm, c.count(14, 6))
                pool.tensor_tensor(r2[:, 0], ve2[:, s, 0], minus_half[:], ALU.pow).then_inc(ln2_norm, 1)
                pool.wait_ge(ln2_norm, c.count(14, 7))
                pool.tensor_tensor(nr2[:, 0], nm2[:, s], r2[:, 0], ALU.mult).then_inc(ln2_norm, 1)
                pool.tensor_scalar(up2[:], r2[:, 0], 1.0, None, ALU.add).then_inc(ln2_norm, 1)
                wait_apart(pool, ln2_norm, c.count(14, 9), pool_passed)
                normalise(base[:, s], base[:, s], up2, nr2[:, 0], ln2_norm)
                pool.wait_ge(ln2_norm, c.count(14, 13))
                pool.tensor_tensor(base[:, s], base[:, s], b2_bc[:].unsqueeze(1).to_broadcast([P, TT, D]), ALU.add
                                   ).then_inc(ln2_norm, 1)

            def slot(t):
                mixed, nxt = t - 1, t + 1
                if not (t - 2).exists:
                    if mixed.exists:
                        o_times_c(mixed)
                        pool.wait_ge(ln1_norm, t.count(6, 6))
                    if first(t):
                        pool.wait_ge(ln1_norm, 6)
                    ln1(nxt)
                    input_times_z(t)
                    if mixed.exists:
                        rrms_of(mixed)
                        pool.wait_ge(w2_rounded, 1)
                        pool.tensor_tensor(w2_lo[:], w2_f, w2_hi[:].bitcast(F32), ALU.subtract).then_inc(w2_ready, 1)
                        ln2_g(mixed)
                    return
                base_last = early_h(t)
                if not base_last:
                    ln2_base(t - 2)
                if nxt.exists:
                    ln1(nxt)
                if t.exists and base_last:
                    input_times_z(t)
                if mixed.exists:
                    o_times_c(mixed)
                if t.exists and not base_last:
                    input_times_z(t)
                if base_last:
                    ln2_base(t - 2)
                if mixed.exists:
                    rrms_of(mixed)
                    ln2_g(mixed)

            pool.memset(ident[:], 0.0).then_inc(ident_ready, 1)
            pool.wait_ge(ident_ready, 1)
            pool.affine_select(out=ident[:], in_=ident[:], compare_op=ALU.not_equal, fill=1.0, base=0,
                               pattern=[[-1, P]], channel_multiplier=1).then_inc(ident_ready, 1)
            pool.wait_ge(half_ready, 1)
            ln1(Chunk(0))
            pool.wait_ge(row_in, 32)
            pool.tensor_scalar(b2_bc[:], b2_bc[:], 0.5, 0.0, ALU.mult, ALU.add).then_inc(half_ready, 1)
            pool.wait_ge(half_ready, 2)
            run_slots(pool, slot)


def kernel(L0_attn_x, L0_attn_W, L0_attn_b, L0_attn_input_bias, L0_attn_scale, L0_ffn_ln_gamma, L0_ffn_ln_beta,
           L0_ffn_fc1_q, L0_ffn_fc1_scales, L0_ffn_fc1_bias, L0_ffn_fc2_q, L0_ffn_fc2_scales, L0_ffn_fc2_bias):
    import numpy as np
    import concourse.bacc as bacc
    from concourse.bass_utils import run_bass_kernel_spmd

    def by_partition(v):
        return np.asarray(v).reshape(-1, P).T

    arrays = {
        "x": np.asarray(L0_attn_x),
        "w_gates": np.asarray(L0_attn_W),
        "cols": np.ascontiguousarray(np.concatenate([by_partition(v) for v in (
            L0_attn_b, L0_attn_input_bias, L0_ffn_ln_gamma, L0_ffn_ln_beta, L0_ffn_fc1_bias)], axis=1)),
        "scale_row": np.asarray(L0_attn_scale),
        "fc1_q": np.asarray(L0_ffn_fc1_q),
        "fc1_scales": np.asarray(L0_ffn_fc1_scales),
        "fc2_q": np.asarray(L0_ffn_fc2_q),
        "fc2_scales": np.asarray(L0_ffn_fc2_scales),
        "b2_row": np.asarray(L0_ffn_fc2_bias),
    }
    nc = bacc.Bacc("TRN2", target_bir_lowering=False, num_devices=1)
    args = [nc.dram_tensor(n, a.shape, mybir.dt.from_np(a.dtype), kind="ExternalInput").ap() for n, a in arrays.items()]
    out = nc.dram_tensor("out", (SEQS, STEPS, D), F32, kind="ExternalOutput").ap()
    layer(nc, *args, out)
    r = run_bass_kernel_spmd(nc, [arrays], core_ids=[0])
    return r.results[0]["out"]
```
